# Optimizing a Trainium2 kernel written in Bass

```python
import numpy as np
import jax
import jax.numpy as jnp

def _softmax(x, axis=-1):
    return jax.nn.softmax(x, axis=axis)

def _gelu(x):
    return jax.nn.gelu(x, approximate=True)

def _silu(x):
    return jax.nn.silu(x)

def _sigmoid(x):
    return jax.nn.sigmoid(x)

def _layernorm(x, axis=-1, eps=1e-05):
    m = jnp.mean(x, axis=axis, keepdims=True)
    v = jnp.var(x, axis=axis, keepdims=True)
    return (x - m) / jnp.sqrt(v + eps)

def _scatter_add(tgt, idx, src, axis=0):
    return tgt.at[idx].add(src)

def _segment_sum(src, seg, n):
    return jax.ops.segment_sum(src, seg, n)
kernel_name = 'mk_pixart_resid_d1_seqx_r4_7f76ab'

def setup_inputs(seed: int=0):
    np.random.seed(seed)
    _w = jnp.asarray

    def _rec_inputs():
        import jax
        import jax.numpy as jnp
        _rk = jax.random.key(seed)
        x = -0.0002928 + 1 * jax.random.normal(jax.random.fold_in(_rk, 1), (32, 128, 512), jnp.float32)
        _lenS = 128 - jax.random.randint(jax.random.fold_in(_rk, 7), (32,), 0, max(1, 128 // 4) + 1, jnp.int32)
        _lenS2 = 128 - jax.random.randint(jax.random.fold_in(_rk, 8), (32,), 0, max(1, 128 // 4) + 1, jnp.int32)
        _ctx_2048P = jax.random.normal(jax.random.fold_in(_rk, 11), (32, 16, 512), jnp.float32)
        _ctx_2048c = jax.random.dirichlet(jax.random.fold_in(_rk, 511), 0.3 * jnp.ones((16,), jnp.float32), (32, 128))
        _ctx_2048t = jnp.einsum('bsk,bkd->bsd', _ctx_2048c, _ctx_2048P)
        _ctx_2048t = _ctx_2048t * jax.lax.rsqrt(jnp.mean(jnp.square(_ctx_2048t)) + 1e-12) * 0.953939
        ctx_2048 = -1.39393e-06 + 0.999914 * (_ctx_2048t + 0.3 * jax.random.normal(jax.random.fold_in(_rk, 611), (32, 128, 512), jnp.float32))
        itok_B_779_1933 = jax.random.randint(jax.random.fold_in(_rk, 12), (32,), 779, 1934, jnp.int32)
        return (x, ctx_2048, itok_B_779_1933)
    x, ctx_2048, itok_B_779_1933 = _rec_inputs()

    def _L0_xcond_setup():
        import jax, jax.numpy as jnp
        import numpy as np
        NUM_HEADS = 8
        HEAD_DIM = 64
        AVG_K_LENGTH = 20
        SCALE = 1.0 / (HEAD_DIM ** 0.5 * float(np.log(AVG_K_LENGTH)))
        key = jax.random.key(seed)
        k1, k2, k3, k4 = jax.random.split(key, 4)
        B, HD, LQ, LK = (4, NUM_HEADS * HEAD_DIM, 512, 512)
        q = jax.random.normal(k1, (B, HD, LQ), dtype=jnp.float32)
        k = jax.random.normal(k2, (B, HD, LK), dtype=jnp.float32)
        v = jax.random.normal(k3, (B, HD, LK), dtype=jnp.float32)
        k_length = jax.random.randint(k4, (B,), 128, LK + 1, dtype=jnp.int32)
        return {'q': q, 'k': k, 'v': v, 'k_length': k_length}
    _L0_xcond_all = _L0_xcond_setup()
    _L0_xcond_in = {k: v for k, v in _L0_xcond_all.items() if k in ()}
    del _L0_xcond_all

    def _L0_ffn_setup():
        import jax, jax.numpy as jnp
        import numpy as np
        B, S, D, I, E, K = (4, 256, 512, 256, 8, 2)
        key = jax.random.key(seed)
        ks = jax.random.split(key, 7)

        def w(k, shape, fan_in):
            return jax.random.normal(k, shape, dtype=jnp.float32) * fan_in ** (-0.5)
        return {'hidden_states': jax.random.normal(ks[0], (B, S, D), dtype=jnp.float32), 'router_w': w(ks[1], (D, E), D), 'gate_up_w': w(ks[2], (E, D, 2 * I), D), 'down_w': w(ks[3], (E, I, D), I), 'shared_gate_w': w(ks[4], (D, I), D), 'shared_up_w': w(ks[5], (D, I), D), 'shared_down_w': w(ks[6], (I, D), I)}
    _L0_ffn_all = _L0_ffn_setup()
    _L0_ffn_in = {k: v for k, v in _L0_ffn_all.items() if k in ('router_w', 'gate_up_w', 'down_w', 'shared_gate_w', 'shared_up_w', 'shared_down_w')}
    del _L0_ffn_all
    return {'x': x, 'ctx_2048': ctx_2048, 'itok_B_779_1933': itok_B_779_1933, 'L0_ffn_router_w': _L0_ffn_in['router_w'], 'L0_ffn_gate_up_w': _L0_ffn_in['gate_up_w'], 'L0_ffn_down_w': _L0_ffn_in['down_w'], 'L0_ffn_shared_gate_w': _L0_ffn_in['shared_gate_w'], 'L0_ffn_shared_up_w': _L0_ffn_in['shared_up_w'], 'L0_ffn_shared_down_w': _L0_ffn_in['shared_down_w']}

def reference(x, ctx_2048, itok_B_779_1933, L0_ffn_router_w, L0_ffn_gate_up_w, L0_ffn_down_w, L0_ffn_shared_gate_w, L0_ffn_shared_up_w, L0_ffn_shared_down_w):
    import jax
    import jax.numpy as jnp

    def _L0_xcond_ref(q, k, v, k_length):
        import jax, jax.numpy as jnp
        import numpy as np
        NUM_HEADS = 8
        HEAD_DIM = 64
        AVG_K_LENGTH = 20
        SCALE = 1.0 / (HEAD_DIM ** 0.5 * float(np.log(AVG_K_LENGTH)))
        b, hd, lq = q.shape
        lk = k.shape[-1]
        d = hd // NUM_HEADS
        qh = q.reshape(b, NUM_HEADS, d, lq)
        kh = k.reshape(b, NUM_HEADS, d, lk)
        vh = v.reshape(b, NUM_HEADS, d, lk)
        s = SCALE * jnp.log(k_length.astype(jnp.float32))[:, None, None, None]
        attn = jnp.einsum('bhdq,bhdk->bhqk', qh, kh)
        attn = jax.nn.softmax(s * attn, axis=-1)
        out = jnp.einsum('bhqk,bhdk->bhdq', attn, vh)
        return out.reshape(b, hd, lq)

    def _L0_ffn_ref(hidden_states, router_w, gate_up_w, down_w, shared_gate_w, shared_up_w, shared_down_w):
        import jax, jax.numpy as jnp
        import numpy as np
        B, S, D, I, E, K = (4, 256, 512, 256, 8, 2)
        Bb, Ss, Dd = hidden_states.shape
        x = hidden_states.reshape(-1, Dd)
        T = x.shape[0]
        shared = jax.nn.silu(x @ shared_gate_w) * (x @ shared_up_w) @ shared_down_w
        logits = x @ router_w
        top_val, top_idx = jax.lax.top_k(logits, K)
        probs = jnp.zeros_like(logits).at[jnp.arange(T)[:, None], top_idx].set(jax.nn.sigmoid(top_val))
        xin = probs.T[:, :, None] * x[None]
        gu = jnp.einsum('etd,edf->etf', xin, gate_up_w)
        gate, up = jnp.split(gu, 2, axis=-1)
        h = jax.nn.silu(gate) * up
        expert_out = jnp.einsum('eti,eid->etd', h, down_w)
        combined = shared + expert_out.sum(axis=0)
        return combined.reshape(Bb, Ss, Dd)
    x = x + _L0_xcond_ref(_layernorm(x, axis=-1), ctx_2048, ctx_2048, itok_B_779_1933)
    x = x + _L0_ffn_ref(_layernorm(x, axis=-1), L0_ffn_router_w, L0_ffn_gate_up_w, L0_ffn_down_w, L0_ffn_shared_gate_w, L0_ffn_shared_up_w, L0_ffn_shared_down_w)
    return x

_drawn_inputs = setup_inputs


def setup_inputs(seed=0):
    import zlib

    import numpy as np

    out = dict(_drawn_inputs(seed))
    spreads = {}
    factors = {}
    for name, (base, spread) in spreads.items():
        noise = np.random.default_rng([zlib.crc32(name.encode()), seed]).standard_normal(out[name].shape)
        drawn = base * np.exp(spread * noise) if base else spread * noise
        out[name] = jnp.asarray(drawn.astype(out[name].dtype))
    for name, factor in factors.items():
        out[name] = (out[name] * factor).astype(out[name].dtype)
    return out
```

```python
from contextlib import ExitStack

import numpy as np

import concourse.bass as bass
from concourse import mybir

F32 = mybir.dt.float32
BF16 = mybir.dt.bfloat16
I32 = mybir.dt.int32
U32 = mybir.dt.uint32
ALU = mybir.AluOpType
ACT = mybir.ActivationFunctionType
AX = mybir.AxisListType

P = 128
B, ROWS, L = 32, 128, 512
H, DH = 8, 16
SETS, HS = 2, 4
KT = L // P
GROUPS = SETS * KT
UNITS = GROUPS * HS
PAIRS = H * KT // 2
PARTS = 3
Q_PART = (0, 1, 2, 0, 1, 0)
K_PART = (2, 1, 0, 1, 0, 0)
Q_SLOT = (0, 1, 2)
K_SLOT = (5, 4, 3)
STACK = len(Q_PART) * DH
SLOT = 32
LN_EPS = 1e-5
SCALE = 1.0 / (64 ** 0.5 * float(np.log(20)))

T = B * ROWS
D = L
E, F = 8, 256
TOP = 2
DC = D // P
FC = F // P
TILES = T * TOP // P + E - 1


def live(n, count=B):
    return 0 <= n < count if isinstance(n, int) else True


def run_steps(eng, step, first, lo, hi, last):
    for b in range(first, lo):
        step(b, b % 2)
    with eng.Fori(0, (hi - lo) // 2) as i:
        b = eng.snap(i * 2 + lo)
        step(b, lo % 2)
        step(b + 1, 1 - lo % 2)
    for b in range(hi, last + 1):
        step(b, b % 2)


def at(dram, b):
    if isinstance(b, int):
        return dram[b]
    n = "abcdef"[:len(dram.shape) - 1]
    return dram[bass.ds(b, 1)].rearrange(f"z {' '.join(n)} -> (z {n[0]}) {' '.join(n[1:])}")


def wait_apart(nc, dve, semaphore, value, mark):
    dve.wait_ge(semaphore, value)
    nc.vector.tensor_copy(mark[0:1, 1:2], mark[0:1, 0:1])


def landed(t, k, inc=16, ring=2):
    return inc // ring * t + (inc - inc // ring * k)


def drain_ring(eng, sems, count, inc=16):
    for k, s in enumerate(sems):
        eng.wait_ge(s, inc * len(range(k, count, len(sems))))


def count_of(eng, value):
    return value if isinstance(value, int) else eng.snap(value)


def attention(nc, x, ctx_in, lengths, x2_dram, keep):
    scr = lambda name, shape, dt: nc.dram_tensor(name, shape, dt, kind="Internal").ap()
    split_dram = scr("split_dram", [B, 2 * PARTS, DH, H, L], BF16)
    o_dram = scr("o_dram", [B, H, SLOT, L], F32)
    rden_dram = scr("rden_dram", [B, H, L], F32)

    with ExitStack() as ctx:
        sb = lambda name, shape, dt: ctx.enter_context(nc.sbuf_tensor(name, shape, dt))
        ps = lambda name, shape, dt: ctx.enter_context(nc.psum_tensor(name, shape, dt))
        sem = lambda name: ctx.enter_context(nc.semaphore(name))

        x_in = sb("x_in", [P, 2, L], F32)
        ctx_sb = sb("ctx_sb", [P, 2, L], F32)
        q_norm = sb("q_norm", [P, 2, L], F32)
        split_sb = sb("split_sb", [P, 2, 2 * PARTS, L], BF16)
        q_rest = sb("q_rest", [P, L], F32)
        k_rest = sb("k_rest", [P, L], F32)
        stack = sb("stack", [P, 2, 2, H, L], BF16)
        v_t = sb("v_t", [P, 2, KT, H, SLOT], F32)
        probs = sb("probs", [P, 2, HS, L], F32)
        o_sb = sb("o_sb", [P, 2, SETS, L], F32)
        den = sb("den", [P, 2, H * L // P], F32)
        rden = sb("rden", [P, 2, H * L // P], F32)
        num = sb("num", [P, 2, L], F32)
        rden_rows = sb("rden_rows", [P, 2, L], F32)
        x_again = sb("x_again", [P, 2, L], F32)
        neg_max = sb("neg_max", [P, 2, H * KT], F32)
        nm_split = sb("nm_split", [P, SETS, PARTS, HS * KT], BF16)
        nm_rest = sb("nm_rest", [P, HS * KT], F32)
        nm_rows = sb("nm_rows", [PARTS * HS * KT, SETS, P], BF16)
        ident_bf = sb("ident_bf", [P, P], BF16)
        stats = sb("stats", [P, 6], F32)
        moments = sb("moments", [P, 2], F32)
        mark = sb("mark", [1, 2], F32)
        var_eps = sb("var_eps", [P, 1], F32)
        power = sb("power", [P, 1], F32)
        rstd = sb("rstd", [P, 1], F32)
        q_scale = sb("q_scale", [P, 1], F32)
        len_i = sb("len_i", [P, B], I32)
        len_f = sb("len_f", [P, B], F32)
        len_ln = sb("len_ln", [P, B], F32)
        len_scale = sb("len_scale", [P, B], F32)
        zeros = sb("zeros", [P, TILES * D // B], F32)
        ident = keep["ident"]

        smax_ps = ps("smax_ps", [P, 2, 2, L], F32)
        st_ps = ps("st_ps", [P, 2, L], F32)
        o_ps = ps("o_ps", [P, L], F32)
        turn_ps = ps("turn_ps", [P, L], F32)

        consts = sem("consts")
        shift_ones = sem("shift_ones")
        len_loaded = sem("len_loaded")
        len_ready = sem("len_ready")
        x_loaded = [sem(f"x_loaded{k}") for k in range(2)]
        ctx_loaded = [sem(f"ctx_loaded{k}") for k in range(2)]
        norm_steps = sem("norm_steps")
        rstd_ready = sem("rstd_ready")
        q_normed = sem("q_normed")
        hi_ready = sem("hi_ready")
        split_steps = sem("split_steps")
        k_split_done = sem("k_split_done")
        q_split_done = sem("q_split_done")
        split_written = sem("split_written")
        stack_loaded = [sem(f"stack_loaded{s}") for s in range(SETS)]
        nm_loaded = [sem(f"nm_loaded{s}") for s in range(SETS)]
        v_turned = sem("v_turned")
        v_copied = sem("v_copied")
        smax_done = sem("smax_done")
        max_done = sem("max_done")
        nm_first = sem("nm_first")
        nm_steps = sem("nm_steps")
        nm_split_done = sem("nm_split_done")
        nm_turned = sem("nm_turned")
        nm_copied = sem("nm_copied")
        st_done = sem("st_done")
        exp_done = sem("exp_done")
        pv_done = sem("pv_done")
        o_copied = sem("o_copied")
        o_written = sem("o_written")
        den_loaded = sem("den_loaded")
        rden_ready = sem("rden_ready")
        rden_written = sem("rden_written")
        parts_loaded = [sem(f"parts_loaded{k}") for k in range(2)]
        mixed = sem("mixed")
        x2_ready = sem("x2_ready")
        x2_written = [sem(f"x2_written{k}") for k in range(2)]
        zeros_written = sem("zeros_written")

        block = ctx.enter_context(nc.Block())

        @block.sync
        def _(sp):
            sp.dma_start(len_i[:, :], bass.AP(lengths.tensor, 0, [[0, P], [1, B]])).then_inc(len_loaded, 16)

            def load(t, p):
                if live(t - 2):
                    sp.wait_ge(q_normed, t - 1)
                sp.dma_start(x_in[:, p], at(x, t).rearrange("(h d) f -> d h f", h=H)).then_inc(x_loaded[p], 16)
                if live(t - 2):
                    sp.wait_ge(v_turned, t - 1)
                    sp.wait_ge(k_split_done, t - 1)
                sp.dma_start(ctx_sb[:, p], at(ctx_in, t).rearrange("(h d) f -> d h f", h=H))\
                    .then_inc(ctx_loaded[p], 16)

            def write_split(t, p):
                sp.wait_ge(k_split_done, t + 1)
                sp.wait_ge(q_split_done, t + 1)
                sp.dma_start(at(split_dram, t).rearrange("j d h f -> (d h) j f"), split_sb[:, p])\
                    .then_inc(split_written, 16)

            def load_stack(t, p, s):
                written = count_of(sp, 16 * t + 16)
                if live(t - 2):
                    sp.wait_ge(st_done, UNITS * (t - 2) + UNITS // 2 * (s + 1))
                sp.wait_ge(split_written, written)
                row = 0
                for run in (3, 2, 1):
                    src = at(split_dram, t)[:, :, HS * s:HS * (s + 1), :]\
                        .rearrange("(a t) d h f -> t d a h f", t=run)
                    sp.dma_start(stack[row:row + run * DH, p, :, HS * s:HS * (s + 1), :],
                                 src[:, :, ::2 * PARTS // run - 1]).then_inc(stack_loaded[s], 16)
                    row += run * DH

            def load_shift(t, p, s):
                sp.wait_ge(nm_copied, 2 * t + s + 1)
                sp.dma_start(stack[STACK:STACK + PARTS, p, 0, HS * s:HS * (s + 1), :], nm_rows[:, s, :])\
                    .then_inc(nm_loaded[s], 16)

            def write_o(t, p):
                sp.wait_ge(o_copied, 2 * t + 2)
                sp.dma_start(at(o_dram, t).rearrange("(s j) r f -> (j r) s f", s=SETS), o_sb[:, p])\
                    .then_inc(o_written, 16)

            def load_den(t, p):
                sp.wait_ge(o_written, 16 * t + 16)
                sp.dma_start(den[:, p], at(o_dram, t)[:, DH, :].rearrange("h (c w) -> h c w", c=P // H))\
                    .then_inc(den_loaded, 16)

            def write_rden(t, p):
                sp.wait_ge(rden_ready, t + 1)
                sp.dma_start(at(rden_dram, t), rden[:, p]).then_inc(rden_written, 16)

            def load_parts(t, p):
                if live(t - 2):
                    sp.wait_ge(x2_written[p], landed(t - 2, p))
                sp.dma_start(num[:, p], at(o_dram, t)[:, 0:DH, :]).then_inc(parts_loaded[p], 16)
                sp.dma_start(x_again[:, p], at(x, t)).then_inc(parts_loaded[p], 16)
                sp.wait_ge(rden_written, 16 * t + 16)
                sp.dma_start(rden_rows[:, p], at(rden_dram, t).rearrange("h (o f) -> h o f", o=1)
                             .broadcast_to([H, DH, L])).then_inc(parts_loaded[p], 16)

            def write_x2(t, p):
                sp.wait_ge(x2_ready, t + 1)
                sp.dma_start(at(x2_dram, t), x_again[:, p]).then_inc(x2_written[p], 16)

            def clear_rows(t):
                if isinstance(t, int) and t == 0:
                    sp.wait_ge(consts, 6)
                sp.dma_start(at(keep["rows_dram"].rearrange("(b r) d -> b r d", b=B), t), zeros[:, :])\
                    .then_inc(zeros_written, 16)

            loads = {b: [] for b in (0, 1, 2, 3, 4, 29, 30, 31, 32)}
            for n, load_of in enumerate(keep["weight_loads"]):
                loads[list(loads)[n % len(loads)]].append(load_of)

            def step(b, p):
                if live(b + 1):
                    load_stack(b + 1, 1 - p, 1)
                if live(b - 3):
                    write_x2(b - 3, 1 - p)
                if live(b - 2):
                    write_rden(b - 2, p)
                if live(b - 1):
                    write_o(b - 1, 1 - p)
                if live(b):
                    load_shift(b, p, 1)
                if live(b - 2):
                    load_parts(b - 2, p)
                if live(b - 1):
                    load_den(b - 1, 1 - p)
                if live(b + 3):
                    load(b + 3, 1 - p)
                if live(b):
                    clear_rows(b)
                if live(b + 2):
                    write_split(b + 2, p)
                    load_stack(b + 2, p, 0)
                if live(b + 1):
                    load_shift(b + 1, 1 - p, 0)
                for dst, src in loads.get(b, ()) if isinstance(b, int) else ():
                    sp.dma_start(dst, src).then_inc(keep["weights_loaded"], 16)

            run_steps(sp, step, -3, 5, 29, 34)
            drain_ring(sp, x2_written, B)
            sp.wait_ge(zeros_written, 16 * B)

        @block.gpsimd
        def _(pool):
            nc.gpsimd.memset(ident[:, :], 0.0).then_inc(consts, 1)
            nc.gpsimd.memset(v_t[:, :], 0.0).then_inc(consts, 1)
            nc.gpsimd.memset(zeros[:, :], 0.0).then_inc(consts, 1)
            nc.gpsimd.memset(power[:, :], -0.5).then_inc(consts, 1)
            pool.wait_ge(consts, 4)
            nc.gpsimd.affine_select(out=ident[:, :], in_=ident[:, :], compare_op=ALU.not_equal, fill=1.0,
                                    base=0, pattern=[[-1, P]], channel_multiplier=1).then_inc(consts, 1)
            nc.gpsimd.memset(v_t[:, :, :, :, DH:DH + 1], 1.0).then_inc(consts, 1)

            def split(t, p, src, slot, rest, hi_count, done):
                n = 4 * t + (0 if done is k_split_done else 2)
                first, second, third = (split_sb[:, p, j] for j in slot)
                pool.wait_ge(hi_ready, hi_count)
                nc.gpsimd.tensor_tensor(second, src[:, p], first, ALU.subtract).then_inc(split_steps, 1)
                if live(t - 1):
                    pool.wait_ge(done, t)
                nc.gpsimd.tensor_tensor(rest[:, :], src[:, p], first, ALU.subtract).then_inc(split_steps, 1)
                pool.wait_ge(split_steps, n + 2)
                nc.gpsimd.tensor_tensor(third, rest[:, :], second, ALU.subtract).then_inc(done, 1)

            def split_max(t, p, s):
                n = 2 * t + s
                value = neg_max[:, p, HS * KT * s:HS * KT * (s + 1)]
                pool.wait_ge(nm_first, n + 1)
                nc.gpsimd.tensor_tensor(nm_split[:, s, 1], value, nm_split[:, s, 0], ALU.subtract)\
                    .then_inc(nm_steps, 1)
                if not (isinstance(n, int) and n == 0):
                    pool.wait_ge(nm_split_done, n)
                nc.gpsimd.tensor_tensor(nm_rest[:, :], value, nm_split[:, s, 0], ALU.subtract)\
                    .then_inc(nm_steps, 1)
                pool.wait_ge(nm_steps, 2 * n + 2)
                nc.gpsimd.tensor_tensor(nm_split[:, s, 2], nm_rest[:, :], nm_split[:, s, 1], ALU.subtract)\
                    .then_inc(nm_split_done, 1)

            def residual(t, p):
                pool.wait_ge(parts_loaded[p], landed(t, p, 48))
                nc.gpsimd.tensor_tensor(num[:, p], num[:, p], rden_rows[:, p], ALU.mult).then_inc(mixed, 1)
                pool.wait_ge(mixed, t + 1)
                nc.gpsimd.tensor_tensor(x_again[:, p], num[:, p], x_again[:, p], ALU.add).then_inc(x2_ready, 1)

            def step(b, p):
                if live(b):
                    split_max(b, p, 1)
                if live(b + 2):
                    pool.wait_ge(norm_steps, 4 * (b + 2) + 3)
                    nc.gpsimd.tensor_tensor(rstd[:, :], var_eps[:, :], power[:, :], ALU.pow).then_inc(rstd_ready, 1)
                    split(b + 2, p, ctx_sb, K_SLOT, k_rest, 2 * (b + 2) + 1, k_split_done)
                    split(b + 2, p, q_norm, Q_SLOT, q_rest, 2 * (b + 2) + 2, q_split_done)
                if live(b + 1):
                    split_max(b + 1, 1 - p, 0)
                if live(b - 2):
                    residual(b - 2, p)

            run_steps(pool, step, -2, 2, 30, 33)

        @block.vector
        def _(dve):
            nc.vector.memset(mark[:, :], 0.0)
            nc.vector.memset(stack[STACK:STACK + PARTS, :, 1, :, :], 1.0).then_inc(shift_ones, 1)
            dve.wait_ge(consts, 6)
            nc.vector.tensor_copy(ident_bf[:, :], ident[:, :]).then_inc(shift_ones, 1)
            dve.wait_ge(len_loaded, 16)
            nc.vector.tensor_copy(len_f[:, :], len_i[:, :]).then_inc(len_ready, 1)
            dve.wait_ge(len_ready, 2)
            nc.vector.tensor_scalar(len_scale[:, :], len_ln[:, :], SCALE, None, ALU.mult).then_inc(len_ready, 1)
            dve.wait_ge(len_ready, 3)

            def k_first(t, p):
                dve.wait_ge(ctx_loaded[p], landed(t, p))
                if live(t - 2):
                    dve.wait_ge(split_written, 16 * (t - 1))
                nc.vector.tensor_copy(split_sb[:, p, K_SLOT[0]], ctx_sb[:, p]).then_inc(hi_ready, 1)

            def norm_stats(t, p):
                dve.wait_ge(x_loaded[p], landed(t, p))
                nc.vector.bn_stats(stats[:, :], x_in[:, p]).then_inc(norm_steps, 1)

            def norm_moments(t, p):
                wait_apart(nc, dve, norm_steps, 4 * t + 1, mark)
                nc.vector.bn_aggr(moments[:, :], stats[:, :]).then_inc(norm_steps, 1)

            def norm_var(t, p):
                dve.wait_ge(norm_steps, 4 * t + 2)
                nc.vector.tensor_scalar(var_eps[:, :], moments[:, 1:2], LN_EPS, None, ALU.add)\
                    .then_inc(norm_steps, 1)

            def norm_scale(t, p):
                dve.wait_ge(rstd_ready, t + 1)
                col = len_scale[:, t:t + 1] if isinstance(t, int) else len_scale[:, bass.ds(t, 1)]
                nc.vector.tensor_tensor(q_scale[:, :], rstd[:, :], col, ALU.mult).then_inc(norm_steps, 1)

            def norm_apply(t, p):
                dve.wait_ge(norm_steps, 4 * t + 4)
                if live(t - 2):
                    dve.wait_ge(q_split_done, t - 1)
                nc.vector.tensor_scalar(q_norm[:, p], x_in[:, p], moments[:, 0:1], q_scale[:, :],
                                        ALU.subtract, ALU.mult).then_inc(q_normed, 1)

            def q_first(t, p):
                dve.wait_ge(q_normed, t + 1)
                nc.vector.tensor_copy(split_sb[:, p, Q_SLOT[0]], q_norm[:, p]).then_inc(hi_ready, 1)

            def invert(t, p):
                dve.wait_ge(den_loaded, 16 * t + 16)
                if live(t - 2):
                    dve.wait_ge(rden_written, 16 * (t - 1))
                nc.vector.reciprocal(rden[:, p], den[:, p]).then_inc(rden_ready, 1)

            def row_max(t, p, i):
                dve.wait_ge(smax_done, PAIRS * t + i + 1)
                nc.vector.tensor_reduce(neg_max[:, p, 2 * i:2 * i + 2], smax_ps[:, i % 2], AX.X, ALU.max,
                                        negate=True).then_inc(max_done, 1)

            def max_first(t, p, s):
                if not (isinstance(t, int) and t == 0):
                    dve.wait_ge(nm_turned, 2 * t + s - 1)
                dve.wait_ge(max_done, PAIRS * t + PAIRS // 2 * (s + 1))
                nc.vector.tensor_copy(nm_split[:, s, 0], neg_max[:, p, HS * KT * s:HS * KT * (s + 1)])\
                    .then_inc(nm_first, 1)

            between = {0: (k_first, norm_stats), 1: (norm_moments, norm_var), 3: (norm_scale, norm_apply),
                       4: (q_first,)}

            def step(b, p):
                for i in range(PAIRS):
                    if live(b + 1):
                        row_max(b + 1, 1 - p, i)
                    if live(b + 1) and i % (PAIRS // 2) == PAIRS // 2 - 1:
                        max_first(b + 1, 1 - p, i // (PAIRS // 2))
                    for part in between.get(i, ()) if live(b + 2) else ():
                        part(b + 2, p)
                    if i == 12 and live(b - 1):
                        invert(b - 1, 1 - p)

            run_steps(dve, step, -2, 3, 29, 32)

        @block.scalar
        def _(act):
            act.wait_ge(len_ready, 1)
            nc.scalar.activation(len_ln[:, :], len_f[:, :], ACT.Ln).then_inc(len_ready, 1)

            def copy_v(t, p):
                act.wait_ge(v_turned, t + 1)
                if live(t - 2):
                    act.wait_ge(pv_done, GROUPS * (t - 1))
                else:
                    act.wait_ge(consts, 6)
                nc.scalar.activation(v_t[:, p, :, :, 0:DH], turn_ps[:, :].rearrange(
                    "k (t d h) -> k t h d", t=KT, h=H), ACT.Copy).then_inc(v_copied, 1)

            def copy_nm(t, s):
                act.wait_ge(nm_turned, 2 * t + s + 1)
                if live(t - 1):
                    act.wait_ge(nm_loaded[s], 16 * t)
                nc.scalar.activation(nm_rows[:, s], turn_ps[0:PARTS * HS * KT, 0:P], ACT.Copy)\
                    .then_inc(nm_copied, 1)

            def exponentials(t, s, g, j):
                u = UNITS * t + HS * (KT * s + g) + j
                act.wait_ge(st_done, u + 1)
                if j == 0 and not (isinstance(t, int) and t == 0 and s == 0 and g < 2):
                    act.wait_ge(pv_done, GROUPS * t + KT * s + g - 1)
                nc.scalar.activation(probs[:, g % 2, j], st_ps[:, j % 2], ACT.Exp).then_inc(exp_done, 1)

            def copy_o(t, p, s):
                act.wait_ge(pv_done, GROUPS * t + KT * (s + 1))
                if live(t - 2):
                    act.wait_ge(o_written, 16 * (t - 1))
                nc.scalar.activation(o_sb[:, p, s], o_ps[:, :], ACT.Copy).then_inc(o_copied, 1)

            def step(b, p):
                for s in range(SETS):
                    for g in range(KT):
                        for j in range(HS):
                            if live(b):
                                exponentials(b, s, g, j)
                            if g == 0 and j == 3:
                                if s == 0 and live(b - 1):
                                    copy_o(b - 1, 1 - p, 1)
                                if s == 1 and live(b):
                                    copy_o(b, p, 0)
                            if g == 1 and j == 1:
                                if s == 0 and live(b):
                                    copy_nm(b, 1)
                                if s == 1 and live(b + 1):
                                    copy_nm(b + 1, 0)
                            if g == 3 and j == 1 and s == 0 and live(b + 1):
                                copy_v(b + 1, 1 - p)

            run_steps(act, step, -1, 3, 31, 32)

        @block.tensor
        def _(pe):
            pe.wait_ge(consts, 6)
            pe.wait_ge(shift_ones, 2)

            def turn_free(n_v, n_nm):
                for s, n in ((v_copied, n_v), (nm_copied, n_nm)):
                    if not (isinstance(n, int) and n <= 0):
                        pe.wait_ge(s, n)

            def turn_v(t, p):
                turn_free(t, 2 * t)
                pe.wait_ge(ctx_loaded[p], landed(t, p))
                for k in range(KT):
                    last = nc.tensor.transpose(turn_ps[:, k * P:(k + 1) * P], ctx_sb[:, p, k * P:(k + 1) * P],
                                               ident[:, :])
                last.then_inc(v_turned, 1)

            def turn_nm(t, s):
                pe.wait_ge(nm_split_done, 2 * t + s + 1)
                turn_free(t + 1, 2 * t + s)
                nc.tensor.matmul(turn_ps[0:PARTS * HS * KT, 0:P], nm_split[:, s].rearrange("p a c -> p (a c)"),
                                 ident_bf[:, :], start=True, stop=True).then_inc(nm_turned, 1)

            def scores_for_max(t, p, h, pair):
                i = 2 * h + pair
                if h % HS == 0 and pair == 0:
                    pe.wait_ge(stack_loaded[h // HS], 48 * (t + 1))
                if not (isinstance(t, int) and t == 0 and i < 2):
                    pe.wait_ge(max_done, PAIRS * t + i - 1)
                for c in range(2):
                    q0 = (2 * pair + c) * P
                    last = nc.tensor.matmul(smax_ps[:, i % 2, c], stack[0:STACK, p, 0, h, q0:q0 + P],
                                            stack[0:STACK, p, 1, h, :], start=True, stop=True)
                last.then_inc(smax_done, 1)

            def scores(t, p, s, g, j):
                u = UNITS * t + HS * (KT * s + g) + j
                h = HS * s + j
                if g == 0 and j == 0:
                    pe.wait_ge(nm_loaded[s], 16 * (t + 1))
                if not (isinstance(u, int) and u < 2):
                    pe.wait_ge(exp_done, u - 1)
                nc.tensor.matmul(st_ps[:, j % 2], stack[0:STACK + PARTS, p, 1, h, g * P:(g + 1) * P],
                                 stack[0:STACK + PARTS, p, 0, h, :], start=True, stop=True).then_inc(st_done, 1)

            def attend(t, p, s, g, half):
                n = GROUPS * t + KT * s + g
                if half == 0:
                    if g == 0:
                        pe.wait_ge(v_copied, t + 1)
                        if not (isinstance(t, int) and t == 0 and s == 0):
                            pe.wait_ge(o_copied, 2 * t + s)
                    pe.wait_ge(exp_done, HS * n + HS)
                cols = slice(half * L // 2, (half + 1) * L // 2)
                for j in range(HS):
                    last = nc.tensor.matmul(o_ps[SLOT * j:SLOT * (j + 1), cols], v_t[:, p, g, HS * s + j, :],
                                            probs[:, g % 2, j, cols], start=(g == 0 and half == 0),
                                            stop=(g == KT - 1 and half == 1),
                                            tile_position=(0, SLOT * j))
                if half == 1:
                    last.then_inc(pv_done, 1)

            def step(b, p):
                for s in range(SETS):
                    for g in range(KT):
                        h = HS * s + g
                        for j in range(HS):
                            if live(b):
                                scores(b, p, s, g, j)
                            if j % 2 == 0:
                                if live(b + 1):
                                    scores_for_max(b + 1, 1 - p, h, j // 2)
                            elif h > 0:
                                if live(b):
                                    attend(b, p, (h - 1) // KT, (h - 1) % KT, j // 2)
                            elif live(b - 1):
                                attend(b - 1, 1 - p, 1, KT - 1, j // 2)
                        if g == 0 and s == 0 and live(b):
                            turn_nm(b, 1)
                        if g == 0 and s == 1 and live(b + 1):
                            turn_nm(b + 1, 0)
                        if g == 2 and s == 0 and live(b + 1):
                            turn_v(b + 1, 1 - p)

            run_steps(pe, step, -1, 1, 31, 32)


def route(nc, x2_dram, xn_dram, xt_dram, keep):
    with ExitStack() as ctx:
        sb = lambda name, shape, dt: ctx.enter_context(nc.sbuf_tensor(name, shape, dt))
        ps = lambda name, shape, dt: ctx.enter_context(nc.psum_tensor(name, shape, dt))
        sem = lambda name: ctx.enter_context(nc.semaphore(name))

        x2_in = sb("r_x2_in", [P, 2, D], F32)
        xn = sb("r_xn", [P, 2, D], F32)
        xt = sb("r_xt", [P, 2, DC, P], F32)
        stats = sb("r_stats", [P, 6], F32)
        moments = sb("r_moments", [P, 2], F32)
        mark = sb("r_mark", [1, 2], F32)
        var_eps = sb("r_var_eps", [P, 1], F32)
        power = sb("r_power", [P, 1], F32)
        rstd = sb("r_rstd", [P, 1], F32)
        logits = sb("r_logits", [P, 2, E], F32)
        top_val = sb("r_top_val", [P, 2, 8], F32)
        top_idx = sb("r_top_idx", [P, 2, 8], U32)
        turn_ps = ps("r_turn_ps", [P, 2, D], F32)
        logit_ps = ps("r_logit_ps", [P, 2, 512], F32)

        x2_loaded = [sem(f"x2_loaded{k}") for k in range(2)]
        steps = sem("r_norm_steps")
        power_ready = sem("r_power_ready")
        rstd_ready = sem("r_rstd_ready")
        normed = sem("r_normed")
        xn_written = [sem(f"xn_written{k}") for k in range(2)]
        turned = sem("r_turned")
        xt_copied = sem("r_xt_copied")
        xt_written = [sem(f"xt_written{k}") for k in range(2)]
        logits_done = sem("logits_done")
        logits_copied = sem("logits_copied")
        top_steps = sem("top_steps")
        top_kept = sem("top_kept")

        block = ctx.enter_context(nc.Block())

        @block.sync
        def _(sp):
            def load(t, p):
                if live(t - 2):
                    sp.wait_ge(normed, t - 1)
                sp.dma_start(x2_in[:, p], at(x2_dram, t)).then_inc(x2_loaded[p], 16)

            def write(t, p):
                sp.wait_ge(normed, t + 1)
                sp.dma_start(at(xn_dram, t), xn[:, p]).then_inc(xn_written[p], 16)
                sp.wait_ge(xt_copied, t + 1)
                sp.dma_start(at(xt_dram, t), xt[:, p]).then_inc(xt_written[p], 16)

            def step(b, p):
                if live(b + 2):
                    load(b + 2, p)
                if live(b):
                    write(b, p)

            run_steps(sp, step, -2, 0, 30, 31)
            drain_ring(sp, xn_written, B)
            drain_ring(sp, xt_written, B)

        @block.gpsimd
        def _(pool):
            nc.gpsimd.memset(power[:, :], -0.5).then_inc(power_ready, 1)
            pool.wait_ge(power_ready, 1)

            def step(t, p):
                pool.wait_ge(steps, 3 * t + 3)
                nc.gpsimd.tensor_tensor(rstd[:, :], var_eps[:, :], power[:, :], ALU.pow).then_inc(rstd_ready, 1)

            run_steps(pool, step, 0, 0, 32, 31)

        @block.vector
        def _(dve):
            nc.vector.memset(mark[:, :], 0.0)

            def norm(t, p):
                dve.wait_ge(x2_loaded[p], landed(t, p))
                nc.vector.bn_stats(stats[:, :], x2_in[:, p]).then_inc(steps, 1)
                wait_apart(nc, dve, steps, 3 * t + 1, mark)
                nc.vector.bn_aggr(moments[:, :], stats[:, :]).then_inc(steps, 1)
                dve.wait_ge(steps, 3 * t + 2)
                nc.vector.tensor_scalar(var_eps[:, :], moments[:, 1:2], LN_EPS, None, ALU.add).then_inc(steps, 1)
                if live(t - 2):
                    dve.wait_ge(xn_written[p], landed(t - 2, p))
                    dve.wait_ge(turned, t - 1)
                dve.wait_ge(rstd_ready, t + 1)
                nc.vector.tensor_scalar(xn[:, p], x2_in[:, p], moments[:, 0:1], rstd[:, :],
                                        ALU.subtract, ALU.mult).then_inc(normed, 1)

            def choose(t, p):
                wait_apart(nc, dve, logits_copied, t + 1, mark)
                nc.vector.max(top_val[:, p], logits[:, p]).then_inc(top_steps, 1)
                wait_apart(nc, dve, top_steps, 2 * t + 1, mark)
                nc.vector.max_index(top_idx[:, p], top_val[:, p], logits[:, p]).then_inc(top_steps, 1)
                dve.wait_ge(top_steps, 2 * t + 2)
                col = slice(t, t + 1) if isinstance(t, int) else bass.ds(t, 1)
                nc.vector.tensor_copy(keep["top_val"][:, col, :], top_val[:, p:p + 1, 0:TOP]).then_inc(top_kept, 1)
                nc.vector.tensor_copy(keep["top_idx"][:, col, :], top_idx[:, p:p + 1, 0:TOP]).then_inc(top_kept, 1)

            def step(b, p):
                if live(b + 1):
                    norm(b + 1, 1 - p)
                if live(b - 1):
                    choose(b - 1, 1 - p)

            run_steps(dve, step, -1, 1, 31, 32)

        @block.scalar
        def _(act):
            def copy_xt(t, p):
                act.wait_ge(turned, t + 1)
                if live(t - 2):
                    act.wait_ge(xt_written[p], landed(t - 2, p))
                    act.wait_ge(logits_done, t - 1)
                nc.scalar.activation(xt[:, p], turn_ps[:, p].rearrange("k (c t) -> k c t", c=DC), ACT.Copy)\
                    .then_inc(xt_copied, 1)

            def copy_logits(t, p):
                act.wait_ge(logits_done, t + 1)
                if live(t - 2):
                    act.wait_ge(top_steps, 2 * (t - 1))
                nc.scalar.activation(logits[:, p], logit_ps[:, p, 0:E], ACT.Copy).then_inc(logits_copied, 1)

            def step(b, p):
                if live(b):
                    copy_xt(b, p)
                if live(b - 1):
                    copy_logits(b - 1, 1 - p)

            run_steps(act, step, 0, 4, 32, 32)

        @block.tensor
        def _(pe):
            def turn(t, p):
                pe.wait_ge(normed, t + 1)
                if live(t - 2):
                    pe.wait_ge(xt_copied, t - 1)
                for c in range(DC):
                    last = nc.tensor.transpose(turn_ps[:, p, c * P:(c + 1) * P], xn[:, p, c * P:(c + 1) * P],
                                               keep["ident"][:, :])
                last.then_inc(turned, 1)

            def router(t, p):
                if t is first:
                    pe.wait_ge(keep["weights_loaded"], keep["weights_count"])
                pe.wait_ge(xt_copied, t + 1)
                if live(t - 2):
                    pe.wait_ge(logits_copied, t - 1)
                for c in range(DC):
                    last = nc.tensor.matmul(logit_ps[:, p, 0:E], xt[:, p, c], keep["router"][:, c],
                                            start=(c == 0), stop=(c == DC - 1))
                last.then_inc(logits_done, 1)

            first = 0

            def step(b, p):
                if live(b):
                    turn(b, p)
                if live(b - 1):
                    router(b - 1, 1 - p)

            run_steps(pe, step, 0, 4, 32, 32)


def plan(nc, keep):
    with ExitStack() as ctx:
        sb = lambda name, shape, dt: ctx.enter_context(nc.sbuf_tensor(name, shape, dt))
        ps = lambda name, shape, dt: ctx.enter_context(nc.psum_tensor(name, shape, dt))
        sem = lambda name: ctx.enter_context(nc.semaphore(name))

        MAXT = T // P
        iota_e = sb("p_iota_e", [P, E], I32)
        iota_k = sb("p_iota_k", [P, MAXT], I32)
        iota_t = sb("p_iota_t", [P, TILES], I32)
        num_e = sb("p_num_e", [P, 1, E], F32)
        num_k = sb("p_num_k", [P, 1, MAXT], F32)
        num_t = sb("p_num_t", [P, TILES, 1], F32)
        ones = sb("p_ones", [P, P], F32)
        before = sb("p_before", [P, P], F32)
        chosen = sb("p_chosen", [P, TOP, B, E], F32)
        either = sb("p_either", [P, B, E], F32)
        count = sb("p_count", [P, B, E], F32)
        upto = sb("p_upto", [P, 2, B, E], F32)
        place = sb("p_place", [P, 2, B, E], F32)
        placed = sb("p_placed", [P, TOP, B, E], F32)
        pos = sb("p_pos", [P, TOP, B], F32)
        over = sb("p_over", [P, E, MAXT], F32)
        tiles = sb("p_tiles", [P, E], F32)
        ends = sb("p_ends", [P, 2, E], F32)
        starts = sb("p_starts", [P, 1, E], F32)
        passed = sb("p_passed", [P, TILES, E], F32)
        owner = sb("p_owner", [P, TILES], F32)
        rank_ps = ps("p_rank_ps", [P, 512], F32)
        count_ps = ps("p_count_ps", [P, 512], F32)

        iotas = sem("iotas")
        masks = sem("masks")
        chain = sem("plan_chain")
        ranked = sem("ranked")
        prob_done = sem("prob_done")
        block = ctx.enter_context(nc.Block())

        @block.gpsimd
        def _(pool):
            nc.gpsimd.iota(iota_e[:, :], pattern=[[1, E]], base=0, channel_multiplier=0).then_inc(iotas, 1)
            nc.gpsimd.iota(iota_k[:, :], pattern=[[P, MAXT]], base=0, channel_multiplier=0).then_inc(iotas, 1)
            nc.gpsimd.iota(iota_t[:, :], pattern=[[1, TILES]], base=0, channel_multiplier=0).then_inc(iotas, 1)
            nc.gpsimd.memset(ones[:, :], 1.0).then_inc(masks, 1)
            nc.gpsimd.memset(before[:, :], 1.0).then_inc(masks, 1)
            pool.wait_ge(masks, 2)
            nc.gpsimd.affine_select(out=before[:, :], in_=before[:, :], compare_op=ALU.is_gt, fill=0.0,
                                    base=0, pattern=[[1, P]], channel_multiplier=-1).then_inc(masks, 1)

        @block.scalar
        def _(act):
            nc.scalar.activation(keep["prob"][:, :, :], keep["top_val"][:, :, :], ACT.Sigmoid).then_inc(prob_done, 1)
            act.wait_ge(prob_done, 1)

        @block.tensor
        def _(pe):
            pe.wait_ge(masks, 3)
            pe.wait_ge(chain, 6)
            rows = either[:, :, :].rearrange("p b e -> p (b e)")
            nc.tensor.matmul(rank_ps[:, 0:B * E], before[:, :], rows, start=True, stop=True)
            nc.tensor.matmul(count_ps[:, 0:B * E], ones[:, :], rows, start=True, stop=True).then_inc(ranked, 1)

        @block.vector
        def _(dve):
            done = [0]

            def then(instruction):
                done[0] += 1
                instruction.then_inc(chain, 1)
                dve.wait_ge(chain, done[0])

            V = nc.vector
            dve.wait_ge(iotas, 3)
            then(V.tensor_copy(num_e[:, 0, :], iota_e[:, :]))
            then(V.tensor_copy(num_k[:, 0, :], iota_k[:, :]))
            then(V.tensor_copy(num_t[:, :, 0], iota_t[:, :]))
            for k in range(TOP):
                then(V.tensor_tensor(chosen[:, k], keep["top_idx"][:, :, k:k + 1].broadcast_to([P, B, E]),
                                     num_e[:, :, :].broadcast_to([P, B, E]), ALU.is_equal))
            then(V.tensor_tensor(either[:, :, :], chosen[:, 0], chosen[:, 1], ALU.add))
            dve.wait_ge(ranked, 1)
            then(V.tensor_copy(count[:, :, :], count_ps[:, 0:B * E].rearrange("p (b e) -> p b e", b=B)))
            then(V.tensor_copy(upto[:, 0], count[:, :, :]))
            now, shift = 0, 1
            while shift < B:
                then(V.tensor_tensor(upto[:, 1 - now, shift:], upto[:, now, shift:], upto[:, now, :B - shift],
                                     ALU.add))
                then(V.tensor_copy(upto[:, 1 - now, :shift], upto[:, now, :shift]))
                now, shift = 1 - now, 2 * shift
            total = upto[:, now, B - 1:B, :].rearrange("p o e -> p e o")
            then(V.tensor_tensor(over[:, :, :], total.broadcast_to([P, E, MAXT]),
                                 num_k[:, :, :].broadcast_to([P, E, MAXT]), ALU.is_gt))
            then(V.tensor_reduce(tiles[:, :], over[:, :, :], AX.X, ALU.add))
            then(V.tensor_copy(ends[:, 0], tiles[:, :]))
            cur, shift = 0, 1
            while shift < E:
                then(V.tensor_tensor(ends[:, 1 - cur, shift:], ends[:, cur, shift:], ends[:, cur, :E - shift],
                                     ALU.add))
                then(V.tensor_copy(ends[:, 1 - cur, :shift], ends[:, cur, :shift]))
                cur, shift = 1 - cur, 2 * shift
            then(V.tensor_tensor(starts[:, 0, :], ends[:, cur], tiles[:, :], ALU.subtract))
            then(V.tensor_scalar(starts[:, 0, :], starts[:, 0, :], float(P), None, ALU.mult))
            then(V.tensor_tensor(place[:, 0], upto[:, now], count[:, :, :], ALU.subtract))
            then(V.tensor_tensor(place[:, 1], place[:, 0], starts[:, :, :].broadcast_to([P, B, E]), ALU.add))
            then(V.tensor_tensor(place[:, 0], place[:, 1],
                                 rank_ps[:, 0:B * E].rearrange("p (b e) -> p b e", b=B), ALU.add))
            for k in range(TOP):
                then(V.tensor_tensor(placed[:, k], chosen[:, k], place[:, 0], ALU.mult))
                then(V.tensor_reduce(pos[:, k], placed[:, k], AX.X, ALU.add))
                then(V.tensor_copy(keep["place"][:, :, k], pos[:, k]))
            then(V.tensor_tensor(passed[:, :, :], num_t[:, :, :].broadcast_to([P, TILES, E]),
                                 ends[:, cur:cur + 1, :].broadcast_to([P, TILES, E]), ALU.is_ge))
            then(V.tensor_reduce(owner[:, :], passed[:, :, :], AX.X, ALU.add))
            then(V.tensor_scalar(keep["owner"][:, :], owner[:, :], float(E - 1), None, ALU.min))


def column(t):
    return slice(t, t + 1) if isinstance(t, int) else bass.ds(t, 1)


def shared_and_scatter(nc, x2_dram, xn_dram, xt_dram, acc_dram, down_w, keep):
    rows_dram = keep["rows_dram"]
    with ExitStack() as ctx:
        sb = lambda name, shape, dt: ctx.enter_context(nc.sbuf_tensor(name, shape, dt))
        ps = lambda name, shape, dt: ctx.enter_context(nc.psum_tensor(name, shape, dt))
        sem = lambda name: ctx.enter_context(nc.semaphore(name))

        xt = sb("s_xt", [P, 2, DC, P], F32)
        x2 = sb("s_x2", [P, 2, D], F32)
        xn = sb("s_xn", [P, 2, D], F32)
        gate = sb("s_gate", [P, 2, F], F32)
        hid = sb("s_hid", [P, 2, F], F32)
        hid_t = sb("s_hid_t", [P, 2, FC, P], F32)
        acc = sb("s_acc", [P, 2, D], F32)
        scaled = sb("s_scaled", [P, 2, TOP, D], F32)
        prob = sb("s_prob", [P, 2, TOP], F32)
        place = sb("s_place", [P, 2, TOP], U32)
        gu_ps = ps("s_gu_ps", [P, 2, 2 * F], F32)
        ht_ps = ps("s_ht_ps", [P, 2, 512], F32)
        down_ps = ps("s_down_ps", [P, 2, D], F32)

        xt_loaded = [sem(f"s_xt_loaded{k}") for k in range(2)]
        x2_loaded = [sem(f"s_x2_loaded{k}") for k in range(2)]
        xn_loaded = [sem(f"s_xn_loaded{k}") for k in range(2)]
        gu_done = sem("s_gu_done")
        gated = sem("s_gated")
        hid_done = sem("s_hid_done")
        hid_turned = sem("s_hid_turned")
        hid_copied = sem("s_hid_copied")
        down_done = sem("s_down_done")
        acc_done = sem("s_acc_done")
        acc_written = [sem(f"s_acc_written{k}") for k in range(2)]
        picked = sem("s_picked")
        row_scaled = sem("s_row_scaled")
        scattered = [sem(f"s_scattered{k}") for k in range(2)]

        block = ctx.enter_context(nc.Block())

        @block.sync
        def _(sp):
            def load(t, p):
                if live(t - 2):
                    sp.wait_ge(gu_done, t - 1)
                sp.dma_start(xt[:, p], at(xt_dram, t)).then_inc(xt_loaded[p], 16)
                if live(t - 2):
                    sp.wait_ge(row_scaled, 2 * (t - 1))
                sp.dma_start(xn[:, p], at(xn_dram, t)).then_inc(xn_loaded[p], 16)
                if live(t - 2):
                    sp.wait_ge(acc_done, t - 1)
                sp.dma_start(x2[:, p], at(x2_dram, t)).then_inc(x2_loaded[p], 16)

            def write(t, p):
                sp.wait_ge(acc_done, t + 1)
                sp.dma_start(at(acc_dram, t), acc[:, p]).then_inc(acc_written[p], 16)

            def step(b, p):
                if live(b):
                    write(b, p)
                if live(b + 2):
                    load(b + 2, p)
                if isinstance(b, int) and b == 0:
                    for e in range(E):
                        sp.dma_start(keep["down"][:, e], down_w[e].rearrange("(c p) n -> p c n", p=P))\
                            .then_inc(keep["down_loaded"], 16)

            run_steps(sp, step, -2, 2, 30, 31)
            drain_ring(sp, acc_written, B)
            sp.wait_ge(keep["down_loaded"], 16 * E)

        @block.gpsimd
        def _(pool):
            def scatter(t, p):
                pool.wait_ge(row_scaled, 2 * t + 2)
                for k in range(TOP):
                    nc.gpsimd.indirect_dma_start(
                        out=rows_dram, out_offset=bass.IndirectOffsetOnAxis(ap=place[:, p, k:k + 1], axis=0),
                        in_=scaled[:, p, k], in_offset=None).then_inc(scattered[p], 16)

            for t in range(B):
                scatter(t, t % 2)
            drain_ring(pool, scattered, B, 16 * TOP)

        @block.vector
        def _(dve):
            def scale(t, p):
                if live(t - 2):
                    dve.wait_ge(scattered[p], landed(t - 2, p, 32))
                nc.vector.tensor_copy(prob[:, p:p + 1], keep["prob"][:, column(t), :]).then_inc(picked, 1)
                nc.vector.tensor_copy(place[:, p:p + 1], keep["place"][:, column(t), :]).then_inc(picked, 1)
                dve.wait_ge(xn_loaded[p], landed(t, p))
                dve.wait_ge(picked, 2 * t + 2)
                for k in range(TOP):
                    nc.vector.tensor_scalar(scaled[:, p, k], xn[:, p], prob[:, p, k:k + 1], None, ALU.mult)\
                        .then_inc(row_scaled, 1)

            def hidden(t, p):
                dve.wait_ge(gated, t + 1)
                if live(t - 2):
                    dve.wait_ge(hid_turned, t - 1)
                nc.vector.tensor_tensor(hid[:, p], gate[:, p], gu_ps[:, p, F:], ALU.mult).then_inc(hid_done, 1)

            def accumulate(t, p):
                dve.wait_ge(down_done, t + 1)
                dve.wait_ge(x2_loaded[p], landed(t, p))
                if live(t - 2):
                    dve.wait_ge(acc_written[p], landed(t - 2, p))
                nc.vector.tensor_tensor(acc[:, p], down_ps[:, p], x2[:, p], ALU.add).then_inc(acc_done, 1)

            def step(b, p):
                if live(b):
                    hidden(b, p)
                if live(b - 1):
                    accumulate(b - 1, 1 - p)
                if live(b):
                    scale(b, p)

            run_steps(dve, step, 0, 4, 32, 32)

        @block.scalar
        def _(act):
            def silu(t, p):
                act.wait_ge(gu_done, t + 1)
                if live(t - 2):
                    act.wait_ge(hid_done, t - 1)
                nc.scalar.activation(gate[:, p], gu_ps[:, p, 0:F], ACT.Silu).then_inc(gated, 1)

            def copy_hidden(t, p):
                act.wait_ge(hid_turned, t + 1)
                if live(t - 2):
                    act.wait_ge(down_done, t - 1)
                nc.scalar.activation(hid_t[:, p], ht_ps[:, p, 0:F].rearrange("k (c t) -> k c t", c=FC), ACT.Copy)\
                    .then_inc(hid_copied, 1)

            def step(b, p):
                silu(b, p)
                copy_hidden(b, p)

            run_steps(act, step, 0, 2, 32, 31)

        @block.tensor
        def _(pe):
            def gate_up(t, p):
                pe.wait_ge(xt_loaded[p], landed(t, p))
                if live(t - 2):
                    pe.wait_ge(hid_done, t - 1)
                for c in range(DC):
                    last = nc.tensor.matmul(gu_ps[:, p], xt[:, p, c], keep["shared_gu"][:, c],
                                            start=(c == 0), stop=(c == DC - 1))
                last.then_inc(gu_done, 1)

            def turn_hidden(t, p):
                pe.wait_ge(hid_done, t + 1)
                if live(t - 2):
                    pe.wait_ge(hid_copied, t - 1)
                for c in range(FC):
                    last = nc.tensor.transpose(ht_ps[:, p, c * P:(c + 1) * P], hid[:, p, c * P:(c + 1) * P],
                                               keep["ident"][:, :])
                last.then_inc(hid_turned, 1)

            def down(t, p):
                pe.wait_ge(hid_copied, t + 1)
                if live(t - 2):
                    pe.wait_ge(acc_done, t - 1)
                for c in range(FC):
                    last = nc.tensor.matmul(down_ps[:, p], hid_t[:, p, c], keep["shared_down"][:, c],
                                            start=(c == 0), stop=(c == FC - 1))
                last.then_inc(down_done, 1)

            def step(b, p):
                if live(b):
                    gate_up(b, p)
                if live(b - 1):
                    down(b - 1, 1 - p)
                if live(b):
                    turn_hidden(b, p)

            run_steps(pe, step, 0, 4, 32, 32)


def experts(nc, y_dram, keep):
    rows = keep["rows_dram"].rearrange("(i p) d -> i p d", p=P)
    N = TILES
    with ExitStack() as ctx:
        sb = lambda name, shape, dt: ctx.enter_context(nc.sbuf_tensor(name, shape, dt))
        ps = lambda name, shape, dt: ctx.enter_context(nc.psum_tensor(name, shape, dt))
        sem = lambda name: ctx.enter_context(nc.semaphore(name))

        x = sb("e_x", [P, 2, D], F32)
        xt = sb("e_xt", [P, 2, DC, P], F32)
        gate = sb("e_gate", [P, 2, F], F32)
        hid = sb("e_hid", [P, 2, F], F32)
        hid_t = sb("e_hid_t", [P, 2, FC, P], F32)
        y = sb("e_y", [P, 2, D], F32)
        turn_ps = ps("e_turn_ps", [P, D], F32)
        gu_ps = ps("e_gu_ps", [P, 2, 2 * F], F32)
        ht_ps = ps("e_ht_ps", [P, 2, 512], F32)
        down_ps = ps("e_down_ps", [P, 2, D], F32)

        x_loaded = [sem(f"e_x_loaded{k}") for k in range(2)]
        turned = sem("e_turned")
        xt_copied = sem("e_xt_copied")
        gu_done = sem("e_gu_done")
        gated = sem("e_gated")
        hid_done = sem("e_hid_done")
        hid_turned = sem("e_hid_turned")
        hid_copied = sem("e_hid_copied")
        down_done = sem("e_down_done")
        y_done = sem("e_y_done")
        y_written = [sem(f"e_y_written{k}") for k in range(2)]

        block = ctx.enter_context(nc.Block())

        @block.sync
        def _(sp):
            def step(i, p):
                if live(i + 2, N):
                    if live(i, N):
                        sp.wait_ge(turned, i + 1)
                    sp.dma_start(x[:, p], at(rows, i + 2)).then_inc(x_loaded[p], 16)
                if live(i, N):
                    sp.wait_ge(y_done, i + 1)
                    sp.dma_start(at(y_dram, i), y[:, p]).then_inc(y_written[p], 16)

            run_steps(sp, step, -2, 0, N - 3, N - 1)
            drain_ring(sp, y_written, N)

        @block.vector
        def _(dve):
            def hidden(t, p):
                dve.wait_ge(gated, t + 1)
                if live(t - 2, N):
                    dve.wait_ge(hid_turned, t - 1)
                nc.vector.tensor_tensor(hid[:, p], gate[:, p], gu_ps[:, p, F:], ALU.mult).then_inc(hid_done, 1)

            def copy_hidden(t, p):
                dve.wait_ge(hid_turned, t + 1)
                if live(t - 2, N):
                    dve.wait_ge(down_done, t - 1)
                nc.vector.tensor_copy(hid_t[:, p], ht_ps[:, p, 0:F].rearrange("k (c t) -> k c t", c=FC))\
                    .then_inc(hid_copied, 1)

            def copy_y(t, p):
                dve.wait_ge(down_done, t + 1)
                if live(t - 2, N):
                    dve.wait_ge(y_written[p], landed(t - 2, p))
                nc.vector.tensor_copy(y[:, p], down_ps[:, p]).then_inc(y_done, 1)

            def step(i, p):
                if live(i, N):
                    hidden(i, p)
                if live(i - 1, N):
                    copy_y(i - 1, 1 - p)
                if live(i, N):
                    copy_hidden(i, p)

            run_steps(dve, step, 0, 4, N - 1, N)

        @block.scalar
        def _(act):
            def copy_xt(t, p):
                act.wait_ge(turned, t + 1)
                if live(t - 2, N):
                    act.wait_ge(gu_done, t - 1)
                nc.scalar.activation(xt[:, p], turn_ps[:, :].rearrange("k (c t) -> k c t", c=DC), ACT.Copy)\
                    .then_inc(xt_copied, 1)

            def silu(t, p):
                act.wait_ge(gu_done, t + 1)
                if live(t - 2, N):
                    act.wait_ge(hid_done, t - 1)
                nc.scalar.activation(gate[:, p], gu_ps[:, p, 0:F], ACT.Silu).then_inc(gated, 1)

            def step(i, p):
                if live(i, N):
                    silu(i, p)
                if live(i + 1, N):
                    copy_xt(i + 1, 1 - p)

            run_steps(act, step, -1, 3, N - 2, N - 1)

        @block.tensor
        def _(pe):
            def owner(t):
                return pe.value_load(keep["owner"][0:1, column(t)], min_val=0, max_val=E - 1)

            def turn(t, p):
                pe.wait_ge(x_loaded[p], landed(t, p))
                if live(t - 1, N):
                    pe.wait_ge(xt_copied, t)
                for c in range(DC):
                    last = nc.tensor.transpose(turn_ps[:, c * P:(c + 1) * P], x[:, p, c * P:(c + 1) * P],
                                               keep["ident"][:, :])
                last.then_inc(turned, 1)

            def gate_up(t, p):
                e = owner(t)
                pe.wait_ge(xt_copied, t + 1)
                if live(t - 2, N):
                    pe.wait_ge(hid_done, t - 1)
                for c in range(DC):
                    last = nc.tensor.matmul(gu_ps[:, p], xt[:, p, c],
                                            keep["gate_up"][:, bass.ds(e * (DC * 2 * F) + c * 2 * F, 2 * F)],
                                            start=(c == 0), stop=(c == DC - 1))
                last.then_inc(gu_done, 1)

            def turn_hidden(t, p):
                pe.wait_ge(hid_done, t + 1)
                if live(t - 2, N):
                    pe.wait_ge(hid_copied, t - 1)
                for c in range(FC):
                    last = nc.tensor.transpose(ht_ps[:, p, c * P:(c + 1) * P], hid[:, p, c * P:(c + 1) * P],
                                               keep["ident"][:, :])
                last.then_inc(hid_turned, 1)

            def down(t, p):
                e = owner(t)
                pe.wait_ge(hid_copied, t + 1)
                if live(t - 2, N):
                    pe.wait_ge(y_done, t - 1)
                for c in range(FC):
                    last = nc.tensor.matmul(down_ps[:, p], hid_t[:, p, c],
                                            keep["down_flat"][:, bass.ds(e * (FC * D) + c * D, D)],
                                            start=(c == 0), stop=(c == FC - 1))
                last.then_inc(down_done, 1)

            def step(i, p):
                if live(i, N):
                    gate_up(i, p)
                if live(i + 1, N):
                    turn(i + 1, 1 - p)
                if live(i - 1, N):
                    down(i - 1, 1 - p)
                if live(i, N):
                    turn_hidden(i, p)

            run_steps(pe, step, -1, 4, N - 1, N)


def combine(nc, acc_dram, y_dram, out, keep):
    y_rows = y_dram.rearrange("i p d -> (i p) d")
    with ExitStack() as ctx:
        sb = lambda name, shape, dt: ctx.enter_context(nc.sbuf_tensor(name, shape, dt))
        sem = lambda name: ctx.enter_context(nc.semaphore(name))
        NB = 4
        acc = sb("c_acc", [P, NB, D], F32)
        y = sb("c_y", [P, NB, TOP, D], F32)
        place = sb("c_place", [P, NB, TOP], U32)
        acc_loaded = [sem(f"c_acc_loaded{k}") for k in range(NB)]
        picked = sem("c_picked")
        gathered = [sem(f"c_gathered{k}") for k in range(NB)]
        summed = sem("c_summed")
        out_done = sem("c_out_done")
        out_written = [sem(f"c_out_written{k}") for k in range(NB)]

        block = ctx.enter_context(nc.Block())

        def run(eng, step, first, lo, hi, last):
            for b in range(first, lo):
                step(b, b % NB)
            with eng.Fori(0, (hi - lo) // NB) as i:
                b = eng.snap(i * NB + lo)
                for k in range(NB):
                    step(b + k, (lo + k) % NB)
            for b in range(hi, last + 1):
                step(b, b % NB)

        @block.sync
        def _(sp):
            def step(b, p):
                if live(b + NB - 1):
                    if live(b - 1):
                        sp.wait_ge(out_written[(p + NB - 1) % NB], landed(b - 1, (p + NB - 1) % NB, 16, NB))
                    sp.dma_start(acc[:, (p + NB - 1) % NB], at(acc_dram, b + NB - 1)).then_inc(acc_loaded[(p + NB - 1) % NB], 16)
                if live(b):
                    sp.wait_ge(out_done, b + 1)
                    sp.dma_start(at(out, b), acc[:, p]).then_inc(out_written[p], 16)

            run(sp, step, 1 - NB, 1, 29, 31)
            drain_ring(sp, out_written, B)

        @block.gpsimd
        def _(pool):
            def step(t, p):
                pool.wait_ge(picked, t + 1)
                for k in range(TOP):
                    nc.gpsimd.indirect_dma_start(
                        out=y[:, p, k], out_offset=None, in_=y_rows,
                        in_offset=bass.IndirectOffsetOnAxis(ap=place[:, p, k:k + 1], axis=0))\
                        .then_inc(gathered[p], 16)

            for t in range(B):
                step(t, t % NB)

        @block.vector
        def _(dve):
            def step(b, p):
                if live(b + NB - 1):
                    t, q = b + NB - 1, (p + NB - 1) % NB
                    if live(b - 1):
                        dve.wait_ge(out_done, b)
                    nc.vector.tensor_copy(place[:, q:q + 1], keep["place"][:, column(t), :]).then_inc(picked, 1)
                if live(b):
                    dve.wait_ge(gathered[p], landed(b, p, 32, NB))
                    nc.vector.tensor_tensor(y[:, p, 0], y[:, p, 0], y[:, p, 1], ALU.add).then_inc(summed, 1)
                    dve.wait_ge(acc_loaded[p], landed(b, p, 16, NB))
                    dve.wait_ge(summed, b + 1)
                    nc.vector.tensor_tensor(acc[:, p], acc[:, p], y[:, p, 0], ALU.add).then_inc(out_done, 1)

            run(dve, step, 1 - NB, 1, 29, 31)


def program(nc, x, ctx_2048, itok_B_779_1933, router_w, gate_up_w, down_w, shared_gate_w, shared_up_w,
            shared_down_w, out):
    scr = lambda name, shape: nc.dram_tensor(name, shape, F32, kind="Internal").ap()
    x2_dram = scr("x2_dram", [B, P, D])
    xn_dram = scr("xn_dram", [B, P, D])
    xt_dram = scr("xt_dram", [B, P, DC, P])
    acc_dram = scr("acc_dram", [B, P, D])
    y_dram = scr("y_dram", [TILES, P, D])
    with ExitStack() as ctx:
        sb = lambda name, shape, dt: ctx.enter_context(nc.sbuf_tensor(name, shape, dt))
        gate_up = sb("gate_up", [P, E * DC * 2 * F], F32)
        shared_gu = sb("shared_gu", [P, DC, 2 * F], F32)
        shared_down = sb("shared_down", [P, FC, D], F32)
        router = sb("router", [P, DC, E], F32)
        keep = {
            "rows_dram": scr("rows_dram", [TILES * P, D]),
            "ident": sb("ident", [P, P], F32),
            "router": router,
            "shared_gu": shared_gu,
            "shared_down": shared_down,
            "gate_up": gate_up,
            "weights_loaded": ctx.enter_context(nc.semaphore("weights_loaded")),
            "down_loaded": ctx.enter_context(nc.semaphore("down_loaded")),
        }
        gu_e = gate_up[:, :].rearrange("p (e c n) -> p e c n", e=E, c=DC)
        loads = [(gu_e[:, e], gate_up_w[e].rearrange("(c p) n -> p c n", p=P)) for e in range(E)]
        small = [(shared_gu[:, :, 0:F], shared_gate_w.rearrange("(c p) n -> p c n", p=P)),
                 (shared_gu[:, :, F:], shared_up_w.rearrange("(c p) n -> p c n", p=P)),
                 (shared_down[:, :, :], shared_down_w.rearrange("(c p) n -> p c n", p=P)),
                 (router[:, :, :], router_w.rearrange("(c p) n -> p c n", p=P))]
        keep["weight_loads"] = loads[:3] + small[3:] + loads[3:]
        keep["weight_loads"] = [loads[0], loads[1], loads[2], small[0], small[1], small[2], small[3]] + loads[3:]
        keep["weights_count"] = 16 * len(keep["weight_loads"])
        attention(nc, x, ctx_2048, itok_B_779_1933, x2_dram, keep)
        keep["top_val"] = sb("top_val_all", [P, B, TOP], F32)
        keep["top_idx"] = sb("top_idx_all", [P, B, TOP], F32)
        keep["prob"] = sb("prob_all", [P, B, TOP], F32)
        keep["place"] = sb("place_all", [P, B, TOP], U32)
        keep["owner"] = sb("owner_all", [P, TILES], I32)
        down_flat = sb("down", [P, E * FC * D], F32)
        keep["down_flat"] = down_flat
        keep["down"] = down_flat[:, :].rearrange("p (e c n) -> p e c n", e=E, c=FC)
        route(nc, x2_dram, xn_dram, xt_dram, keep)
        plan(nc, keep)
        shared_and_scatter(nc, x2_dram, xn_dram, xt_dram, acc_dram, down_w, keep)
        experts(nc, y_dram, keep)
        combine(nc, acc_dram, y_dram, out, keep)


_INS = ["x", "ctx_2048", "itok_B_779_1933", "L0_ffn_router_w", "L0_ffn_gate_up_w", "L0_ffn_down_w",
        "L0_ffn_shared_gate_w", "L0_ffn_shared_up_w", "L0_ffn_shared_down_w"]
_OUTS = [((B, ROWS, L), "float32")]


def kernel(**inputs):
    import numpy as _np
    import concourse.bacc as _bacc
    from concourse import mybir as _mybir
    from concourse.bass_utils import run_bass_kernel_spmd as _run

    nc = _bacc.Bacc("TRN2", target_bir_lowering=False, num_devices=1)
    arrays, args = {}, []
    for name in _INS:
        a = _np.ascontiguousarray(inputs[name])
        arrays[f"in_{name}_dram"] = a
        args.append(nc.dram_tensor(f"in_{name}_dram", a.shape, _mybir.dt.from_np(a.dtype), kind="ExternalInput").ap())
    for i, (shape, dtype) in enumerate(_OUTS):
        dt = _mybir.dt.from_np(_np.dtype(dtype))
        args.append(nc.dram_tensor(f"out_{i}_dram", shape, dt, kind="ExternalOutput").ap())
    program(nc, *args)
    r = _run(nc, [arrays], core_ids=[0])
    got = tuple(r.results[0][f"out_{i}_dram"] for i in range(len(_OUTS)))
    return got[0]
```

```python
from contextlib import ExitStack

import numpy as np

import concourse.bass as bass
from concourse import mybir

F32 = mybir.dt.float32
BF16 = mybir.dt.bfloat16
I32 = mybir.dt.int32
U32 = mybir.dt.uint32
ALU = mybir.AluOpType
ACT = mybir.ActivationFunctionType
AX = mybir.AxisListType

P = 128
B, ROWS, L = 32, 128, 512
H, DH = 8, 16
SETS, HS = 2, 4
KT = L // P
GROUPS = SETS * KT
UNITS = GROUPS * HS
PAIRS = H * KT // 2
PARTS = 3
Q_PART = (0, 1, 2, 0, 1, 0)
K_PART = (2, 1, 0, 1, 0, 0)
Q_SLOT = (0, 1, 2)
K_SLOT = (5, 4, 3)
STACK = len(Q_PART) * DH
SLOT = 32
LN_EPS = 1e-5
SCALE = 1.0 / (64 ** 0.5 * float(np.log(20)))

T = B * ROWS
D = L
E, F = 8, 256
TOP = 2
DC = D // P
FC = F // P
TILES = T * TOP // P + E - 1


def live(n, count=B):
    return 0 <= n < count if isinstance(n, int) else True


def run_steps(eng, step, first, lo, hi, last, ring=2):
    for b in range(first, lo):
        step(b, b % ring)
    with eng.Fori(0, (hi - lo) // ring) as i:
        b = eng.snap(i * ring + lo)
        for k in range(ring):
            step(b + k, (lo + k) % ring)
    for b in range(hi, last + 1):
        step(b, b % ring)


def at(dram, b):
    if isinstance(b, int):
        return dram[b]
    n = "abcdef"[:len(dram.shape) - 1]
    return dram[bass.ds(b, 1)].rearrange(f"z {' '.join(n)} -> (z {n[0]}) {' '.join(n[1:])}")


def wait_apart(nc, dve, semaphore, value, mark, slot=1):
    dve.wait_ge(semaphore, value)
    nc.vector.tensor_copy(mark[0:1, slot:slot + 1], mark[0:1, 0:1])


def landed(t, k, inc=16, ring=2):
    return inc // ring * t + (inc - inc // ring * k)


def drain_ring(eng, sems, count, inc=16):
    for k, s in enumerate(sems):
        eng.wait_ge(s, inc * len(range(k, count, len(sems))))


def count_of(eng, value):
    return value if isinstance(value, int) else eng.snap(value)


def attention(nc, x, ctx_in, lengths, x2_dram, keep):
    scr = lambda name, shape, dt: nc.dram_tensor(name, shape, dt, kind="Internal").ap()
    split_dram = scr("split_dram", [B, 2 * PARTS, DH, H, L], BF16)
    o_dram = scr("o_dram", [B, H, SLOT, L], F32)
    rden_dram = scr("rden_dram", [B, H, L], F32)

    with ExitStack() as ctx:
        sb = lambda name, shape, dt: ctx.enter_context(nc.sbuf_tensor(name, shape, dt))
        ps = lambda name, shape, dt: ctx.enter_context(nc.psum_tensor(name, shape, dt))
        sem = lambda name: ctx.enter_context(nc.semaphore(name))

        x_in = sb("x_in", [P, 2, L], F32)
        ctx_sb = sb("ctx_sb", [P, 2, L], F32)
        q_norm = sb("q_norm", [P, 2, L], F32)
        split_sb = sb("split_sb", [P, 2, 2 * PARTS, L], BF16)
        q_rest = sb("q_rest", [P, L], F32)
        k_rest = sb("k_rest", [P, L], F32)
        stack = sb("stack", [P, 2, 2, H, L], BF16)
        v_t = sb("v_t", [P, 2, KT, H, SLOT], F32)
        probs = sb("probs", [P, 2, HS, L], F32)
        o_sb = sb("o_sb", [P, 2, SETS, L], F32)
        den = sb("den", [P, 2, H * L // P], F32)
        rden = sb("rden", [P, 2, H * L // P], F32)
        num = sb("num", [P, 2, L], F32)
        rden_rows = sb("rden_rows", [P, 2, L], F32)
        x_again = sb("x_again", [P, 2, L], F32)
        neg_max = sb("neg_max", [P, 2, H * KT], F32)
        nm_split = sb("nm_split", [P, SETS, PARTS, HS * KT], BF16)
        nm_rest = sb("nm_rest", [P, HS * KT], F32)
        nm_rows = sb("nm_rows", [PARTS * HS * KT, SETS, P], BF16)
        ident_bf = sb("ident_bf", [P, P], BF16)
        stats = sb("stats", [P, 6], F32)
        moments = sb("moments", [P, 2], F32)
        mark = sb("mark", [1, 2], F32)
        var_eps = sb("var_eps", [P, 1], F32)
        power = sb("power", [P, 1], F32)
        rstd = sb("rstd", [P, 1], F32)
        q_scale = sb("q_scale", [P, 1], F32)
        len_i = sb("len_i", [P, B], I32)
        len_f = sb("len_f", [P, B], F32)
        len_ln = sb("len_ln", [P, B], F32)
        len_scale = sb("len_scale", [P, B], F32)
        zeros = sb("zeros", [P, TILES * D // B], F32)
        ident = keep["ident"]

        smax_ps = ps("smax_ps", [P, 2, 2, L], F32)
        st_ps = ps("st_ps", [P, 2, L], F32)
        o_ps = ps("o_ps", [P, L], F32)
        turn_ps = ps("turn_ps", [P, L], F32)

        consts = sem("consts")
        shift_ones = sem("shift_ones")
        len_loaded = sem("len_loaded")
        len_ready = sem("len_ready")
        x_loaded = [sem(f"x_loaded{k}") for k in range(2)]
        ctx_loaded = [sem(f"ctx_loaded{k}") for k in range(2)]
        norm_steps = sem("norm_steps")
        rstd_ready = sem("rstd_ready")
        q_normed = sem("q_normed")
        hi_ready = sem("hi_ready")
        split_steps = sem("split_steps")
        k_split_done = sem("k_split_done")
        q_split_done = sem("q_split_done")
        split_written = sem("split_written")
        stack_loaded = [sem(f"stack_loaded{s}") for s in range(SETS)]
        nm_loaded = [sem(f"nm_loaded{s}") for s in range(SETS)]
        v_turned = sem("v_turned")
        v_copied = sem("v_copied")
        smax_done = sem("smax_done")
        max_done = sem("max_done")
        nm_first = sem("nm_first")
        nm_steps = sem("nm_steps")
        nm_split_done = sem("nm_split_done")
        nm_turned = sem("nm_turned")
        nm_copied = sem("nm_copied")
        st_done = sem("st_done")
        exp_done = sem("exp_done")
        pv_done = sem("pv_done")
        o_copied = sem("o_copied")
        o_written = sem("o_written")
        den_loaded = sem("den_loaded")
        rden_ready = sem("rden_ready")
        rden_written = sem("rden_written")
        parts_loaded = [sem(f"parts_loaded{k}") for k in range(2)]
        mixed = sem("mixed")
        x2_ready = sem("x2_ready")
        x2_written = [sem(f"x2_written{k}") for k in range(2)]
        zeros_written = sem("zeros_written")

        block = ctx.enter_context(nc.Block())

        @block.sync
        def _(sp):
            sp.dma_start(len_i[:, :], bass.AP(lengths.tensor, 0, [[0, P], [1, B]])).then_inc(len_loaded, 16)

            def load(t, p):
                if live(t - 2):
                    sp.wait_ge(q_normed, t - 1)
                sp.dma_start(x_in[:, p], at(x, t).rearrange("(h d) f -> d h f", h=H)).then_inc(x_loaded[p], 16)
                if live(t - 2):
                    sp.wait_ge(v_turned, t - 1)
                    sp.wait_ge(k_split_done, t - 1)
                sp.dma_start(ctx_sb[:, p], at(ctx_in, t).rearrange("(h d) f -> d h f", h=H))\
                    .then_inc(ctx_loaded[p], 16)

            def write_split(t, p):
                sp.wait_ge(k_split_done, t + 1)
                sp.wait_ge(q_split_done, t + 1)
                sp.dma_start(at(split_dram, t).rearrange("j d h f -> (d h) j f"), split_sb[:, p])\
                    .then_inc(split_written, 16)

            def load_stack(t, p, s):
                written = count_of(sp, 16 * t + 16)
                if live(t - 2):
                    sp.wait_ge(st_done, UNITS * (t - 2) + UNITS // 2 * (s + 1))
                sp.wait_ge(split_written, written)
                row = 0
                for run in (3, 2, 1):
                    src = at(split_dram, t)[:, :, HS * s:HS * (s + 1), :]\
                        .rearrange("(a t) d h f -> t d a h f", t=run)
                    sp.dma_start(stack[row:row + run * DH, p, :, HS * s:HS * (s + 1), :],
                                 src[:, :, ::2 * PARTS // run - 1]).then_inc(stack_loaded[s], 16)
                    row += run * DH

            def load_shift(t, p, s):
                sp.wait_ge(nm_copied, 2 * t + s + 1)
                sp.dma_start(stack[STACK:STACK + PARTS, p, 0, HS * s:HS * (s + 1), :], nm_rows[:, s, :])\
                    .then_inc(nm_loaded[s], 16)

            def write_o(t, p):
                sp.wait_ge(o_copied, 2 * t + 2)
                sp.dma_start(at(o_dram, t).rearrange("(s j) r f -> (j r) s f", s=SETS), o_sb[:, p])\
                    .then_inc(o_written, 16)

            def load_den(t, p):
                sp.wait_ge(o_written, 16 * t + 16)
                sp.dma_start(den[:, p], at(o_dram, t)[:, DH, :].rearrange("h (c w) -> h c w", c=P // H))\
                    .then_inc(den_loaded, 16)

            def write_rden(t, p):
                sp.wait_ge(rden_ready, t + 1)
                sp.dma_start(at(rden_dram, t), rden[:, p]).then_inc(rden_written, 16)

            def load_parts(t, p):
                if live(t - 2):
                    sp.wait_ge(x2_written[p], landed(t - 2, p))
                sp.dma_start(num[:, p], at(o_dram, t)[:, 0:DH, :]).then_inc(parts_loaded[p], 16)
                sp.dma_start(x_again[:, p], at(x, t)).then_inc(parts_loaded[p], 16)
                sp.wait_ge(rden_written, 16 * t + 16)
                sp.dma_start(rden_rows[:, p], at(rden_dram, t).rearrange("h (o f) -> h o f", o=1)
                             .broadcast_to([H, DH, L])).then_inc(parts_loaded[p], 16)

            def write_x2(t, p):
                sp.wait_ge(x2_ready, t + 1)
                sp.dma_start(at(x2_dram, t), x_again[:, p]).then_inc(x2_written[p], 16)

            def clear_rows(t):
                if isinstance(t, int) and t == 0:
                    sp.wait_ge(consts, 6)
                sp.dma_start(at(keep["rows_dram"].rearrange("(b r) d -> b r d", b=B), t), zeros[:, :])\
                    .then_inc(zeros_written, 16)

            loads = {b: [] for b in (0, 1, 2, 3, 4, 29, 30, 31, 32)}
            for n, load_of in enumerate(keep["weight_loads"]):
                loads[list(loads)[n % len(loads)]].append(load_of)

            def step(b, p):
                if live(b + 1):
                    load_stack(b + 1, 1 - p, 1)
                if live(b - 3):
                    write_x2(b - 3, 1 - p)
                if live(b - 2):
                    write_rden(b - 2, p)
                if live(b - 1):
                    write_o(b - 1, 1 - p)
                if live(b):
                    load_shift(b, p, 1)
                if live(b - 2):
                    load_parts(b - 2, p)
                if live(b - 1):
                    load_den(b - 1, 1 - p)
                if live(b + 3):
                    load(b + 3, 1 - p)
                if live(b):
                    clear_rows(b)
                if live(b + 2):
                    write_split(b + 2, p)
                    load_stack(b + 2, p, 0)
                if live(b + 1):
                    load_shift(b + 1, 1 - p, 0)
                for dst, src in loads.get(b, ()) if isinstance(b, int) else ():
                    sp.dma_start(dst, src).then_inc(keep["weights_loaded"], 16)

            run_steps(sp, step, -3, 5, 29, 34)
            drain_ring(sp, x2_written, B)
            sp.wait_ge(zeros_written, 16 * B)

        @block.gpsimd
        def _(pool):
            nc.gpsimd.memset(ident[:, :], 0.0).then_inc(consts, 1)
            nc.gpsimd.memset(v_t[:, :], 0.0).then_inc(consts, 1)
            nc.gpsimd.memset(zeros[:, :], 0.0).then_inc(consts, 1)
            nc.gpsimd.memset(power[:, :], -0.5).then_inc(consts, 1)
            pool.wait_ge(consts, 4)
            nc.gpsimd.affine_select(out=ident[:, :], in_=ident[:, :], compare_op=ALU.not_equal, fill=1.0,
                                    base=0, pattern=[[-1, P]], channel_multiplier=1).then_inc(consts, 1)
            nc.gpsimd.memset(v_t[:, :, :, :, DH:DH + 1], 1.0).then_inc(consts, 1)

            def split(t, p, src, slot, rest, hi_count, done):
                n = 4 * t + (0 if done is k_split_done else 2)
                first, second, third = (split_sb[:, p, j] for j in slot)
                pool.wait_ge(hi_ready, hi_count)
                nc.gpsimd.tensor_tensor(second, src[:, p], first, ALU.subtract).then_inc(split_steps, 1)
                if live(t - 1):
                    pool.wait_ge(done, t)
                nc.gpsimd.tensor_tensor(rest[:, :], src[:, p], first, ALU.subtract).then_inc(split_steps, 1)
                pool.wait_ge(split_steps, n + 2)
                nc.gpsimd.tensor_tensor(third, rest[:, :], second, ALU.subtract).then_inc(done, 1)

            def split_max(t, p, s):
                n = 2 * t + s
                value = neg_max[:, p, HS * KT * s:HS * KT * (s + 1)]
                pool.wait_ge(nm_first, n + 1)
                nc.gpsimd.tensor_tensor(nm_split[:, s, 1], value, nm_split[:, s, 0], ALU.subtract)\
                    .then_inc(nm_steps, 1)
                if not (isinstance(n, int) and n == 0):
                    pool.wait_ge(nm_split_done, n)
                nc.gpsimd.tensor_tensor(nm_rest[:, :], value, nm_split[:, s, 0], ALU.subtract)\
                    .then_inc(nm_steps, 1)
                pool.wait_ge(nm_steps, 2 * n + 2)
                nc.gpsimd.tensor_tensor(nm_split[:, s, 2], nm_rest[:, :], nm_split[:, s, 1], ALU.subtract)\
                    .then_inc(nm_split_done, 1)

            def residual(t, p):
                pool.wait_ge(parts_loaded[p], landed(t, p, 48))
                nc.gpsimd.tensor_tensor(num[:, p], num[:, p], rden_rows[:, p], ALU.mult).then_inc(mixed, 1)
                pool.wait_ge(mixed, t + 1)
                nc.gpsimd.tensor_tensor(x_again[:, p], num[:, p], x_again[:, p], ALU.add).then_inc(x2_ready, 1)

            def step(b, p):
                if live(b):
                    split_max(b, p, 1)
                if live(b + 2):
                    pool.wait_ge(norm_steps, 4 * (b + 2) + 3)
                    nc.gpsimd.tensor_tensor(rstd[:, :], var_eps[:, :], power[:, :], ALU.pow).then_inc(rstd_ready, 1)
                    split(b + 2, p, ctx_sb, K_SLOT, k_rest, 2 * (b + 2) + 1, k_split_done)
                    split(b + 2, p, q_norm, Q_SLOT, q_rest, 2 * (b + 2) + 2, q_split_done)
                if live(b + 1):
                    split_max(b + 1, 1 - p, 0)
                if live(b - 2):
                    residual(b - 2, p)

            run_steps(pool, step, -2, 2, 30, 33)

        @block.vector
        def _(dve):
            nc.vector.memset(mark[:, :], 0.0)
            nc.vector.memset(stack[STACK:STACK + PARTS, :, 1, :, :], 1.0).then_inc(shift_ones, 1)
            dve.wait_ge(consts, 6)
            nc.vector.tensor_copy(ident_bf[:, :], ident[:, :]).then_inc(shift_ones, 1)
            dve.wait_ge(len_loaded, 16)
            nc.vector.tensor_copy(len_f[:, :], len_i[:, :]).then_inc(len_ready, 1)
            dve.wait_ge(len_ready, 2)
            nc.vector.tensor_scalar(len_scale[:, :], len_ln[:, :], SCALE, None, ALU.mult).then_inc(len_ready, 1)
            dve.wait_ge(len_ready, 3)

            def k_first(t, p):
                dve.wait_ge(ctx_loaded[p], landed(t, p))
                if live(t - 2):
                    dve.wait_ge(split_written, 16 * (t - 1))
                nc.vector.tensor_copy(split_sb[:, p, K_SLOT[0]], ctx_sb[:, p]).then_inc(hi_ready, 1)

            def norm_stats(t, p):
                dve.wait_ge(x_loaded[p], landed(t, p))
                nc.vector.bn_stats(stats[:, :], x_in[:, p]).then_inc(norm_steps, 1)

            def norm_moments(t, p):
                wait_apart(nc, dve, norm_steps, 4 * t + 1, mark)
                nc.vector.bn_aggr(moments[:, :], stats[:, :]).then_inc(norm_steps, 1)

            def norm_var(t, p):
                dve.wait_ge(norm_steps, 4 * t + 2)
                nc.vector.tensor_scalar(var_eps[:, :], moments[:, 1:2], LN_EPS, None, ALU.add)\
                    .then_inc(norm_steps, 1)

            def norm_scale(t, p):
                dve.wait_ge(rstd_ready, t + 1)
                col = len_scale[:, t:t + 1] if isinstance(t, int) else len_scale[:, bass.ds(t, 1)]
                nc.vector.tensor_tensor(q_scale[:, :], rstd[:, :], col, ALU.mult).then_inc(norm_steps, 1)

            def norm_apply(t, p):
                dve.wait_ge(norm_steps, 4 * t + 4)
                if live(t - 2):
                    dve.wait_ge(q_split_done, t - 1)
                nc.vector.tensor_scalar(q_norm[:, p], x_in[:, p], moments[:, 0:1], q_scale[:, :],
                                        ALU.subtract, ALU.mult).then_inc(q_normed, 1)

            def q_first(t, p):
                dve.wait_ge(q_normed, t + 1)
                nc.vector.tensor_copy(split_sb[:, p, Q_SLOT[0]], q_norm[:, p]).then_inc(hi_ready, 1)

            def invert(t, p):
                dve.wait_ge(den_loaded, 16 * t + 16)
                if live(t - 2):
                    dve.wait_ge(rden_written, 16 * (t - 1))
                nc.vector.reciprocal(rden[:, p], den[:, p]).then_inc(rden_ready, 1)

            def row_max(t, p, i):
                dve.wait_ge(smax_done, PAIRS * t + i + 1)
                nc.vector.tensor_reduce(neg_max[:, p, 2 * i:2 * i + 2], smax_ps[:, i % 2], AX.X, ALU.max,
                                        negate=True).then_inc(max_done, 1)

            def max_first(t, p, s):
                if not (isinstance(t, int) and t == 0):
                    dve.wait_ge(nm_turned, 2 * t + s - 1)
                dve.wait_ge(max_done, PAIRS * t + PAIRS // 2 * (s + 1))
                nc.vector.tensor_copy(nm_split[:, s, 0], neg_max[:, p, HS * KT * s:HS * KT * (s + 1)])\
                    .then_inc(nm_first, 1)

            between = {0: (k_first, norm_stats), 1: (norm_moments, norm_var), 3: (norm_scale, norm_apply),
                       4: (q_first,)}

            def step(b, p):
                for i in range(PAIRS):
                    if live(b + 1):
                        row_max(b + 1, 1 - p, i)
                    if live(b + 1) and i % (PAIRS // 2) == PAIRS // 2 - 1:
                        max_first(b + 1, 1 - p, i // (PAIRS // 2))
                    for part in between.get(i, ()) if live(b + 2) else ():
                        part(b + 2, p)
                    if i == 12 and live(b - 1):
                        invert(b - 1, 1 - p)

            run_steps(dve, step, -2, 3, 29, 32)

        @block.scalar
        def _(act):
            act.wait_ge(len_ready, 1)
            nc.scalar.activation(len_ln[:, :], len_f[:, :], ACT.Ln).then_inc(len_ready, 1)

            def copy_v(t, p):
                act.wait_ge(v_turned, t + 1)
                if live(t - 2):
                    act.wait_ge(pv_done, GROUPS * (t - 1))
                else:
                    act.wait_ge(consts, 6)
                nc.scalar.activation(v_t[:, p, :, :, 0:DH], turn_ps[:, :].rearrange(
                    "k (t d h) -> k t h d", t=KT, h=H), ACT.Copy).then_inc(v_copied, 1)

            def copy_nm(t, s):
                act.wait_ge(nm_turned, 2 * t + s + 1)
                if live(t - 1):
                    act.wait_ge(nm_loaded[s], 16 * t)
                nc.scalar.activation(nm_rows[:, s], turn_ps[0:PARTS * HS * KT, 0:P], ACT.Copy)\
                    .then_inc(nm_copied, 1)

            def exponentials(t, s, g, j):
                u = UNITS * t + HS * (KT * s + g) + j
                act.wait_ge(st_done, u + 1)
                if j == 0 and not (isinstance(t, int) and t == 0 and s == 0 and g < 2):
                    act.wait_ge(pv_done, GROUPS * t + KT * s + g - 1)
                nc.scalar.activation(probs[:, g % 2, j], st_ps[:, j % 2], ACT.Exp).then_inc(exp_done, 1)

            def copy_o(t, p, s):
                act.wait_ge(pv_done, GROUPS * t + KT * (s + 1))
                if live(t - 2):
                    act.wait_ge(o_written, 16 * (t - 1))
                nc.scalar.activation(o_sb[:, p, s], o_ps[:, :], ACT.Copy).then_inc(o_copied, 1)

            def step(b, p):
                for s in range(SETS):
                    for g in range(KT):
                        for j in range(HS):
                            if live(b):
                                exponentials(b, s, g, j)
                            if g == 0 and j == 3:
                                if s == 0 and live(b - 1):
                                    copy_o(b - 1, 1 - p, 1)
                                if s == 1 and live(b):
                                    copy_o(b, p, 0)
                            if g == 1 and j == 1:
                                if s == 0 and live(b):
                                    copy_nm(b, 1)
                                if s == 1 and live(b + 1):
                                    copy_nm(b + 1, 0)
                            if g == 3 and j == 1 and s == 0 and live(b + 1):
                                copy_v(b + 1, 1 - p)

            run_steps(act, step, -1, 3, 31, 32)

        @block.tensor
        def _(pe):
            pe.wait_ge(consts, 6)
            pe.wait_ge(shift_ones, 2)

            def turn_free(n_v, n_nm):
                for s, n in ((v_copied, n_v), (nm_copied, n_nm)):
                    if not (isinstance(n, int) and n <= 0):
                        pe.wait_ge(s, n)

            def turn_v(t, p):
                turn_free(t, 2 * t)
                pe.wait_ge(ctx_loaded[p], landed(t, p))
                for k in range(KT):
                    last = nc.tensor.transpose(turn_ps[:, k * P:(k + 1) * P], ctx_sb[:, p, k * P:(k + 1) * P],
                                               ident[:, :])
                last.then_inc(v_turned, 1)

            def turn_nm(t, s):
                pe.wait_ge(nm_split_done, 2 * t + s + 1)
                turn_free(t + 1, 2 * t + s)
                nc.tensor.matmul(turn_ps[0:PARTS * HS * KT, 0:P], nm_split[:, s].rearrange("p a c -> p (a c)"),
                                 ident_bf[:, :], start=True, stop=True).then_inc(nm_turned, 1)

            def scores_for_max(t, p, h, pair):
                i = 2 * h + pair
                if h % HS == 0 and pair == 0:
                    pe.wait_ge(stack_loaded[h // HS], 48 * (t + 1))
                if not (isinstance(t, int) and t == 0 and i < 2):
                    pe.wait_ge(max_done, PAIRS * t + i - 1)
                for c in range(2):
                    q0 = (2 * pair + c) * P
                    last = nc.tensor.matmul(smax_ps[:, i % 2, c], stack[0:STACK, p, 0, h, q0:q0 + P],
                                            stack[0:STACK, p, 1, h, :], start=True, stop=True)
                last.then_inc(smax_done, 1)

            def scores(t, p, s, g, j):
                u = UNITS * t + HS * (KT * s + g) + j
                h = HS * s + j
                if g == 0 and j == 0:
                    pe.wait_ge(nm_loaded[s], 16 * (t + 1))
                if not (isinstance(u, int) and u < 2):
                    pe.wait_ge(exp_done, u - 1)
                nc.tensor.matmul(st_ps[:, j % 2], stack[0:STACK + PARTS, p, 1, h, g * P:(g + 1) * P],
                                 stack[0:STACK + PARTS, p, 0, h, :], start=True, stop=True).then_inc(st_done, 1)

            def attend(t, p, s, g, half):
                n = GROUPS * t + KT * s + g
                if half == 0:
                    if g == 0:
                        pe.wait_ge(v_copied, t + 1)
                        if not (isinstance(t, int) and t == 0 and s == 0):
                            pe.wait_ge(o_copied, 2 * t + s)
                    pe.wait_ge(exp_done, HS * n + HS)
                cols = slice(half * L // 2, (half + 1) * L // 2)
                for j in range(HS):
                    last = nc.tensor.matmul(o_ps[SLOT * j:SLOT * (j + 1), cols], v_t[:, p, g, HS * s + j, :],
                                            probs[:, g % 2, j, cols], start=(g == 0 and half == 0),
                                            stop=(g == KT - 1 and half == 1),
                                            tile_position=(0, SLOT * j))
                if half == 1:
                    last.then_inc(pv_done, 1)

            def step(b, p):
                for s in range(SETS):
                    for g in range(KT):
                        h = HS * s + g
                        for j in range(HS):
                            if live(b):
                                scores(b, p, s, g, j)
                            if j % 2 == 0:
                                if live(b + 1):
                                    scores_for_max(b + 1, 1 - p, h, j // 2)
                            elif h > 0:
                                if live(b):
                                    attend(b, p, (h - 1) // KT, (h - 1) % KT, j // 2)
                            elif live(b - 1):
                                attend(b - 1, 1 - p, 1, KT - 1, j // 2)
                        if g == 0 and s == 0 and live(b):
                            turn_nm(b, 1)
                        if g == 0 and s == 1 and live(b + 1):
                            turn_nm(b + 1, 0)
                        if g == 2 and s == 0 and live(b + 1):
                            turn_v(b + 1, 1 - p)

            run_steps(pe, step, -1, 1, 31, 32)


def column(t):
    return slice(t, t + 1) if isinstance(t, int) else bass.ds(t, 1)


def route(nc, x2_dram, down_w, keep):
    RING = 4
    with ExitStack() as ctx:
        sb = lambda name, shape, dt: ctx.enter_context(nc.sbuf_tensor(name, shape, dt))
        ps = lambda name, shape, dt: ctx.enter_context(nc.psum_tensor(name, shape, dt))
        sem = lambda name: ctx.enter_context(nc.semaphore(name))

        x2_in = sb("r_x2_in", [P, RING, D], F32)
        xn = sb("r_xn", [P, 2, D], F32)
        xt = sb("r_xt", [P, 2, DC, P], F32)
        stats = sb("r_stats", [P, 6], F32)
        moments = sb("r_moments", [P, 2], F32)
        mark = sb("r_mark", [1, 4], F32)
        var_eps = sb("r_var_eps", [P, 1], F32)
        power = sb("r_power", [P, 1], F32)
        rstd = sb("r_rstd", [P, 1], F32)
        logits = sb("r_logits", [P, 2, E], F32)
        top_val = sb("r_top_val", [P, 2, 8], F32)
        top_idx = sb("r_top_idx", [P, 2, 8], U32)
        turn_ps = ps("r_turn_ps", [P, 2, D], F32)
        logit_ps = ps("r_logit_ps", [P, 2, 512], F32)

        x2_loaded = [sem(f"x2_loaded{k}") for k in range(RING)]
        down_loaded = sem("down_loaded")
        steps = sem("r_norm_steps")
        power_ready = sem("r_power_ready")
        rstd_ready = sem("r_rstd_ready")
        normed = sem("r_normed")
        turned = sem("r_turned")
        xt_copied = sem("r_xt_copied")
        xn_kept = sem("r_xn_kept")
        logits_done = sem("logits_done")
        logits_copied = sem("logits_copied")
        top_steps = sem("top_steps")
        top_kept = sem("top_kept")

        block = ctx.enter_context(nc.Block())

        @block.sync
        def _(sp):
            def step(t, p):
                if live(t - RING):
                    sp.wait_ge(normed, t - RING + 1)
                sp.dma_start(x2_in[:, p], at(x2_dram, t)).then_inc(x2_loaded[p], 16)
                if isinstance(t, int) and 4 <= t < 4 + E:
                    sp.dma_start(keep["down"][:, t - 4], down_w[t - 4].rearrange("(c p) n -> p c n", p=P))\
                        .then_inc(down_loaded, 16)

            run_steps(sp, step, 0, 12, 32, 31, RING)
            sp.wait_ge(down_loaded, 16 * E)

        @block.gpsimd
        def _(pool):
            nc.gpsimd.memset(power[:, :], -0.5).then_inc(power_ready, 1)
            pool.wait_ge(power_ready, 1)

            def step(t, p):
                pool.wait_ge(steps, 3 * t + 3)
                nc.gpsimd.tensor_tensor(rstd[:, :], var_eps[:, :], power[:, :], ALU.pow).then_inc(rstd_ready, 1)

            run_steps(pool, step, 0, 0, 32, 31)

        @block.vector
        def _(dve):
            nc.vector.memset(mark[:, :], 0.0)

            def norm_stats(t, p):
                dve.wait_ge(x2_loaded[p], landed(t, p, 16, RING))
                nc.vector.bn_stats(stats[:, :], x2_in[:, p]).then_inc(steps, 1)

            def norm_moments(t):
                wait_apart(nc, dve, steps, 3 * t + 1, mark)
                nc.vector.bn_aggr(moments[:, :], stats[:, :]).then_inc(steps, 1)

            def norm_var(t):
                dve.wait_ge(steps, 3 * t + 2)
                nc.vector.tensor_scalar(var_eps[:, :], moments[:, 1:2], LN_EPS, None, ALU.add).then_inc(steps, 1)

            def norm_apply(t, p):
                if live(t - 2):
                    dve.wait_ge(xn_kept, t - 1)
                dve.wait_ge(rstd_ready, t + 1)
                nc.vector.tensor_scalar(xn[:, p % 2], x2_in[:, p],
                                        moments[:, 0:1], rstd[:, :], ALU.subtract, ALU.mult).then_inc(normed, 1)

            def top(t, p):
                wait_apart(nc, dve, logits_copied, t + 1, mark, 2)
                nc.vector.max(top_val[:, p], logits[:, p]).then_inc(top_steps, 1)

            def top_index(t, p):
                wait_apart(nc, dve, top_steps, 2 * t + 1, mark, 3)
                nc.vector.max_index(top_idx[:, p], top_val[:, p], logits[:, p]).then_inc(top_steps, 1)

            def keep_top(t, p):
                dve.wait_ge(top_steps, 2 * t + 2)
                nc.vector.tensor_copy(keep["top_val"][:, column(t), :], top_val[:, p:p + 1, 0:TOP])\
                    .then_inc(top_kept, 1)
                nc.vector.tensor_copy(keep["top_idx"][:, column(t), :], top_idx[:, p:p + 1, 0:TOP])\
                    .then_inc(top_kept, 1)

            def step(b, p):
                new, old = live(b + 1), live(b - 2)
                if new:
                    norm_stats(b + 1, (p + 1) % RING)
                if old:
                    top(b - 2, p % 2)
                if new:
                    norm_moments(b + 1)
                if old:
                    top_index(b - 2, p % 2)
                if new:
                    norm_var(b + 1)
                if old:
                    keep_top(b - 2, p % 2)
                if new:
                    norm_apply(b + 1, (p + 1) % RING)

            run_steps(dve, step, -1, 3, 31, 33, RING)

        @block.scalar
        def _(act):
            def copy_xt(t, p):
                act.wait_ge(turned, t + 1)
                if live(t - 2):
                    act.wait_ge(logits_done, t - 1)
                nc.scalar.activation(xt[:, p], turn_ps[:, p].rearrange("k (c t) -> k c t", c=DC), ACT.Copy)\
                    .then_inc(xt_copied, 1)

            def keep_xn(t, p):
                nc.scalar.activation(keep["xn"][:, column(t), :], xn[:, p:p + 1], ACT.Copy).then_inc(xn_kept, 1)

            def copy_logits(t, p):
                act.wait_ge(logits_done, t + 1)
                if live(t - 2):
                    act.wait_ge(top_steps, 2 * (t - 1))
                nc.scalar.activation(logits[:, p], logit_ps[:, p, 0:E], ACT.Copy).then_inc(logits_copied, 1)

            def step(b, p):
                if live(b):
                    copy_xt(b, p)
                    keep_xn(b, p)
                if live(b - 1):
                    copy_logits(b - 1, 1 - p)

            run_steps(act, step, 0, 4, 32, 32)

        @block.tensor
        def _(pe):
            def turn(t, p):
                pe.wait_ge(normed, t + 1)
                if live(t - 2):
                    pe.wait_ge(xt_copied, t - 1)
                for c in range(DC):
                    last = nc.tensor.transpose(turn_ps[:, p, c * P:(c + 1) * P], xn[:, p, c * P:(c + 1) * P],
                                               keep["ident"][:, :])
                last.then_inc(turned, 1)

            def router(t, p):
                if isinstance(t, int) and t == 0:
                    pe.wait_ge(keep["weights_loaded"], keep["weights_count"])
                pe.wait_ge(xt_copied, t + 1)
                if live(t - 2):
                    pe.wait_ge(logits_copied, t - 1)
                for c in range(DC):
                    last = nc.tensor.matmul(logit_ps[:, p, 0:E], xt[:, p, c], keep["router"][:, c],
                                            start=(c == 0), stop=(c == DC - 1))
                last.then_inc(logits_done, 1)

            def step(b, p):
                if live(b):
                    turn(b, p)
                if live(b - 1):
                    router(b - 1, 1 - p)

            run_steps(pe, step, 0, 4, 32, 32)


def dispatch(nc, x2_dram, acc_dram, keep):
    RING = 4
    MAXT = T // P
    PLAN_END = 8
    xn = keep["xn"]
    rows_dram = keep["rows_dram"]
    with ExitStack() as ctx:
        sb = lambda name, shape, dt: ctx.enter_context(nc.sbuf_tensor(name, shape, dt))
        ps = lambda name, shape, dt: ctx.enter_context(nc.psum_tensor(name, shape, dt))
        sem = lambda name: ctx.enter_context(nc.semaphore(name))

        iota_e = sb("p_iota_e", [P, E], I32)
        iota_k = sb("p_iota_k", [P, MAXT], I32)
        iota_t = sb("p_iota_t", [P, TILES], I32)
        num_e = sb("p_num_e", [P, 1, E], F32)
        num_k = sb("p_num_k", [P, 1, MAXT], F32)
        num_t = sb("p_num_t", [P, TILES, 1], F32)
        ones = sb("p_ones", [P, P], BF16)
        before = sb("p_before", [P, P], BF16)
        chosen = sb("p_chosen", [P, TOP, B, E], BF16)
        either = sb("p_either", [P, B, E], BF16)
        count = sb("p_count", [P, B, E], F32)
        upto = sb("p_upto", [P, 2, B, E], F32)
        place = sb("p_place", [P, 2, B, E], F32)
        pos = sb("p_pos", [P, TOP, B], F32)
        over = sb("p_over", [P, E, MAXT], BF16)
        tiles = sb("p_tiles", [P, E], F32)
        ends = sb("p_ends", [P, 2, E], F32)
        starts = sb("p_starts", [P, 1, E], F32)
        passed = sb("p_passed", [P, TILES, E], BF16)
        owner = sb("p_owner", [P, TILES], F32)
        plan_ps = ps("p_plan_ps", [P, 2, B * E], F32)

        x = sb("s_x", [P, 1, D], F32)
        xt = sb("s_xt", [P, DC, P], F32)
        x2 = sb("s_x2", [P, RING, D], F32)
        hid = sb("s_hid", [P, 2, F], F32)
        hid_t = sb("s_hid_t", [P, FC, P], F32)
        scaled = sb("s_scaled", [P, 2, TOP, D], F32)
        turn_ps = ps("s_turn_ps", [P, D], F32)
        gu_ps = ps("s_gu_ps", [P, 2, 2 * F], F32)
        ht_ps = ps("s_ht_ps", [P, 2, 512], F32)
        down_ps = ps("s_down_ps", [P, 2, D], F32)

        iotas = sem("iotas")
        masks = sem("masks")
        chain = sem("plan_chain")
        ranked = sem("ranked")
        prob_done = sem("prob_done")
        x_placed = sem("s_x_placed")
        turned = sem("s_turned")
        xt_copied = sem("s_xt_copied")
        x2_loaded = [sem(f"s_x2_loaded{k}") for k in range(RING)]
        gu_done = sem("s_gu_done")
        gated = sem("s_gated")
        hid_done = sem("s_hid_done")
        hid_turned = sem("s_hid_turned")
        hid_copied = sem("s_hid_copied")
        down_done = sem("s_down_done")
        acc_done = sem("s_acc_done")
        acc_written = [sem(f"s_acc_written{k}") for k in range(RING)]
        row_scaled = sem("s_row_scaled")
        scattered = [sem(f"s_scattered{k}") for k in range(2)]

        block = ctx.enter_context(nc.Block())

        @block.sync
        def _(sp):
            def load(t, p):
                if live(t - RING):
                    sp.wait_ge(acc_written[p], landed(t - RING, p, 16, RING))
                sp.dma_start(x2[:, p], at(x2_dram, t)).then_inc(x2_loaded[p], 16)

            def write(t, p):
                sp.wait_ge(acc_done, t + 1)
                sp.dma_start(at(acc_dram, t), x2[:, p]).then_inc(acc_written[p], 16)

            def step(b, p):
                if live(b):
                    write(b, p)
                if live(b + 3):
                    load(b + 3, (p + 3) % RING)

            run_steps(sp, step, -3, 1, 29, 31, RING)
            drain_ring(sp, acc_written, B)

        @block.gpsimd
        def _(pool):
            nc.gpsimd.iota(iota_e[:, :], pattern=[[1, E]], base=0, channel_multiplier=0).then_inc(iotas, 1)
            nc.gpsimd.iota(iota_k[:, :], pattern=[[P, MAXT]], base=0, channel_multiplier=0).then_inc(iotas, 1)
            nc.gpsimd.iota(iota_t[:, :], pattern=[[1, TILES]], base=0, channel_multiplier=0).then_inc(iotas, 1)
            nc.gpsimd.memset(ones[:, :], 1.0).then_inc(masks, 1)
            nc.gpsimd.memset(before[:, :], 1.0).then_inc(masks, 1)
            pool.wait_ge(masks, 2)
            nc.gpsimd.affine_select(out=before[:, :], in_=before[:, :], compare_op=ALU.is_gt, fill=0.0,
                                    base=0, pattern=[[1, P]], channel_multiplier=-1).then_inc(masks, 1)
            for t in range(B):
                pool.wait_ge(row_scaled, TOP * (t + 1))
                for k in range(TOP):
                    nc.gpsimd.indirect_dma_start(
                        out=rows_dram,
                        out_offset=bass.IndirectOffsetOnAxis(ap=keep["place"][:, t, k:k + 1], axis=0),
                        in_=scaled[:, t % 2, k], in_offset=None).then_inc(scattered[t % 2], 16)
            drain_ring(pool, scattered, B, 16 * TOP)

        @block.vector
        def _(dve):
            V = nc.vector
            done = [0]

            def then(instruction):
                done[0] += 1
                instruction.then_inc(chain, 1)
                dve.wait_ge(chain, done[0])

            def plan_choices():
                dve.wait_ge(iotas, 3)
                then(V.tensor_copy(num_e[:, 0, :], iota_e[:, :]))
                then(V.tensor_copy(num_k[:, 0, :], iota_k[:, :]))
                then(V.tensor_copy(num_t[:, :, 0], iota_t[:, :]))
                for k in range(TOP):
                    then(V.tensor_tensor(chosen[:, k], keep["top_idx"][:, :, k:k + 1].broadcast_to([P, B, E]),
                                         num_e[:, :, :].broadcast_to([P, B, E]), ALU.is_equal))
                then(V.tensor_tensor(either[:, :, :], chosen[:, 0], chosen[:, 1], ALU.add))

            def plan_running_counts():
                dve.wait_ge(ranked, 1)
                counts = plan_ps[:, 1].rearrange("p (b e) -> p b e", b=B)
                then(V.tensor_copy(count[:, :, :], counts))
                then(V.tensor_copy(upto[:, 0], counts))
                now, shift = 0, 1
                while shift < B:
                    then(V.tensor_tensor(upto[:, 1 - now, shift:], upto[:, now, shift:], upto[:, now, :B - shift],
                                         ALU.add))
                    then(V.tensor_copy(upto[:, 1 - now, :shift], upto[:, now, :shift]))
                    now, shift = 1 - now, 2 * shift
                return now

            def plan_tiles(now):
                total = upto[:, now, B - 1:B, :].rearrange("p o e -> p e o")
                then(V.tensor_tensor(over[:, :, :], total.broadcast_to([P, E, MAXT]),
                                     num_k[:, :, :].broadcast_to([P, E, MAXT]), ALU.is_gt))
                then(V.tensor_reduce(tiles[:, :], over[:, :, :], AX.X, ALU.add))

            def plan_ends():
                then(V.tensor_copy(ends[:, 0], tiles[:, :]))
                cur, shift = 0, 1
                while shift < E:
                    then(V.tensor_tensor(ends[:, 1 - cur, shift:], ends[:, cur, shift:],
                                         ends[:, cur, :E - shift], ALU.add))
                    then(V.tensor_copy(ends[:, 1 - cur, :shift], ends[:, cur, :shift]))
                    cur, shift = 1 - cur, 2 * shift
                then(V.tensor_tensor(starts[:, 0, :], ends[:, cur], tiles[:, :], ALU.subtract))
                then(V.tensor_scalar(starts[:, 0, :], starts[:, 0, :], float(P), None, ALU.mult))
                return cur

            def plan_places(now):
                then(V.tensor_tensor(place[:, 0], upto[:, now], count[:, :, :], ALU.subtract))
                then(V.tensor_tensor(place[:, 1], place[:, 0], starts[:, :, :].broadcast_to([P, B, E]), ALU.add))
                then(V.tensor_tensor(place[:, 0], place[:, 1], plan_ps[:, 0].rearrange("p (b e) -> p b e", b=B),
                                     ALU.add))

            def plan_pick(k):
                then(V.tensor_tensor(upto[:, k], chosen[:, k], place[:, 0], ALU.mult))
                then(V.tensor_reduce(pos[:, k], upto[:, k], AX.X, ALU.add))
                then(V.tensor_copy(keep["place"][:, :, k], pos[:, k]))

            def plan_owners(cur):
                then(V.tensor_tensor(passed[:, :, :], num_t[:, :, :].broadcast_to([P, TILES, E]),
                                     ends[:, cur:cur + 1, :].broadcast_to([P, TILES, E]), ALU.is_ge))
                then(V.tensor_reduce(owner[:, :], passed[:, :, :], AX.X, ALU.add))
                then(V.tensor_scalar(keep["owner"][:, :], owner[:, :], float(E - 1), None, ALU.min))

            def scale(t, p):
                if isinstance(t, int) and t == 0:
                    dve.wait_ge(prob_done, 1)
                if live(t - 2):
                    dve.wait_ge(scattered[p], landed(t - 2, p, 32))
                for k in range(TOP):
                    prob = keep["prob"][:, column(t), k:k + 1].rearrange("p o k -> p (o k)")
                    V.tensor_scalar(scaled[:, p, k], xn[:, column(t), :].rearrange("p o d -> p (o d)"), prob,
                                    None, ALU.mult).then_inc(row_scaled, 1)

            def hidden(t, p):
                dve.wait_ge(gated, t + 1)
                V.tensor_tensor(hid[:, p], hid[:, p], gu_ps[:, p, F:], ALU.mult).then_inc(hid_done, 1)

            def accumulate(t, p):
                dve.wait_ge(down_done, t + 1)
                dve.wait_ge(x2_loaded[p], landed(t, p, 16, RING))
                V.tensor_tensor(x2[:, p], x2[:, p], down_ps[:, p % 2], ALU.add).then_inc(acc_done, 1)

            def step(b, p):
                if live(b):
                    hidden(b, p % 2)
                if live(b - 1):
                    accumulate(b - 1, (p - 1) % RING)

            def step_and_scale(b, p):
                step(b, p)
                for k in range(2):
                    scale(2 * b - 2 * PLAN_END + k, k)

            step(0, 0)
            plan_choices()
            step(1, 1)
            step(2, 2)
            now = plan_running_counts()
            step(3, 3)
            plan_tiles(now)
            step(4, 0)
            cur = plan_ends()
            step(5, 1)
            plan_places(now)
            step(6, 2)
            for k in range(TOP):
                plan_pick(k)
            step(7, 3)
            plan_owners(cur)
            run_steps(dve, step_and_scale, PLAN_END, PLAN_END + 4, PLAN_END + 16, PLAN_END + 15, RING)
            run_steps(dve, step, PLAN_END + 16, PLAN_END + 16, 32, 32, RING)

        @block.scalar
        def _(act):
            def copy_xt(t, p):
                act.wait_ge(turned, t + 1)
                if live(t - 1):
                    act.wait_ge(gu_done, t)
                nc.scalar.activation(xt[:, :, :], turn_ps[:, :].rearrange("k (c t) -> k c t", c=DC), ACT.Copy)\
                    .then_inc(xt_copied, 1)

            def place_x(t):
                nc.scalar.activation(x[:, :, :], xn[:, column(t), :], ACT.Copy).then_inc(x_placed, 1)

            def silu(t, p):
                act.wait_ge(gu_done, t + 1)
                if live(t - 2):
                    act.wait_ge(hid_turned, t - 1)
                nc.scalar.activation(hid[:, p], gu_ps[:, p, 0:F], ACT.Silu).then_inc(gated, 1)

            def copy_hidden(t, p):
                act.wait_ge(hid_turned, t + 1)
                if live(t - 1):
                    act.wait_ge(down_done, t)
                nc.scalar.activation(hid_t[:, :, :], ht_ps[:, p, 0:F].rearrange("k (c t) -> k c t", c=FC), ACT.Copy)\
                    .then_inc(hid_copied, 1)

            def step(b, p):
                if live(b):
                    silu(b, p)
                if live(b + 1):
                    copy_xt(b + 1, 1 - p)
                if live(b + 2):
                    place_x(b + 2)
                if live(b):
                    copy_hidden(b, p)

            place_x(0)
            nc.scalar.activation(keep["prob"][:, :, :], keep["top_val"][:, :, :], ACT.Sigmoid).then_inc(prob_done, 1)
            run_steps(act, step, -1, 3, 29, 31)

        @block.tensor
        def _(pe):
            def turn(t, p):
                pe.wait_ge(x_placed, t + 1)
                if live(t - 1):
                    pe.wait_ge(xt_copied, t)
                for c in range(DC):
                    last = nc.tensor.transpose(turn_ps[:, c * P:(c + 1) * P], x[:, 0, c * P:(c + 1) * P],
                                               keep["ident"][:, :])
                last.then_inc(turned, 1)

            def gate_up(t, p):
                pe.wait_ge(xt_copied, t + 1)
                if live(t - 2):
                    pe.wait_ge(hid_done, t - 1)
                for c in range(DC):
                    last = nc.tensor.matmul(gu_ps[:, p], xt[:, c], keep["shared_gu"][:, c],
                                            start=(c == 0), stop=(c == DC - 1))
                last.then_inc(gu_done, 1)

            def turn_hidden(t, p):
                pe.wait_ge(hid_done, t + 1)
                if live(t - 2):
                    pe.wait_ge(hid_copied, t - 1)
                for c in range(FC):
                    last = nc.tensor.transpose(ht_ps[:, p, c * P:(c + 1) * P], hid[:, p, c * P:(c + 1) * P],
                                               keep["ident"][:, :])
                last.then_inc(hid_turned, 1)

            def down(t, p):
                pe.wait_ge(hid_copied, t + 1)
                if live(t - 2):
                    pe.wait_ge(acc_done, t - 1)
                for c in range(FC):
                    last = nc.tensor.matmul(down_ps[:, p], hid_t[:, c], keep["shared_down"][:, c],
                                            start=(c == 0), stop=(c == FC - 1))
                last.then_inc(down_done, 1)

            def rank():
                pe.wait_ge(masks, 3)
                pe.wait_ge(chain, 6)
                flags = either[:, :, :].rearrange("p b e -> p (b e)")
                nc.tensor.matmul(plan_ps[:, 0], before[:, :], flags, start=True, stop=True)
                nc.tensor.matmul(plan_ps[:, 1], ones[:, :], flags, start=True, stop=True).then_inc(ranked, 1)

            def step(b, p):
                if live(b):
                    gate_up(b, p)
                if live(b + 1):
                    turn(b + 1, 1 - p)
                if isinstance(b, int) and b == 2:
                    rank()
                if live(b - 1):
                    down(b - 1, 1 - p)
                if live(b):
                    turn_hidden(b, p)

            run_steps(pe, step, -1, 3, 31, 32)


def experts(nc, y_dram, keep):
    RING = 4
    rows = keep["rows_dram"].rearrange("(i p) d -> i p d", p=P)
    N = TILES
    with ExitStack() as ctx:
        sb = lambda name, shape, dt: ctx.enter_context(nc.sbuf_tensor(name, shape, dt))
        ps = lambda name, shape, dt: ctx.enter_context(nc.psum_tensor(name, shape, dt))
        sem = lambda name: ctx.enter_context(nc.semaphore(name))

        x = sb("e_x", [P, RING, D], F32)
        xt = sb("e_xt", [P, 2, DC, P], F32)
        gate = sb("e_gate", [P, 2, F], F32)
        hid = sb("e_hid", [P, 2, F], F32)
        hid_t = sb("e_hid_t", [P, 2, FC, P], F32)
        y = sb("e_y", [P, 2, D], F32)
        turn_ps = ps("e_turn_ps", [P, D], F32)
        gu_ps = ps("e_gu_ps", [P, 2, 2 * F], F32)
        ht_ps = ps("e_ht_ps", [P, 2, 512], F32)
        down_ps = ps("e_down_ps", [P, 2, D], F32)

        x_loaded = [sem(f"e_x_loaded{k}") for k in range(RING)]
        turned = sem("e_turned")
        xt_copied = sem("e_xt_copied")
        gu_done = sem("e_gu_done")
        gated = sem("e_gated")
        hid_done = sem("e_hid_done")
        hid_turned = sem("e_hid_turned")
        hid_copied = sem("e_hid_copied")
        down_done = sem("e_down_done")
        y_done = sem("e_y_done")
        y_written = [sem(f"e_y_written{k}") for k in range(2)]

        block = ctx.enter_context(nc.Block())

        @block.sync
        def _(sp):
            def step(i, p):
                if live(i + 3, N):
                    if live(i - 1, N):
                        sp.wait_ge(turned, i)
                    sp.dma_start(x[:, (p + 3) % RING], at(rows, i + 3)).then_inc(x_loaded[(p + 3) % RING], 16)
                if live(i, N):
                    sp.wait_ge(y_done, i + 1)
                    sp.dma_start(at(y_dram, i), y[:, p % 2]).then_inc(y_written[p % 2], 16)

            run_steps(sp, step, -3, 4, N - 3, N - 1, RING)
            drain_ring(sp, y_written, N)

        @block.vector
        def _(dve):
            def hidden(t, p):
                dve.wait_ge(gated, t + 1)
                if live(t - 2, N):
                    dve.wait_ge(hid_turned, t - 1)
                nc.vector.tensor_tensor(hid[:, p], gate[:, p], gu_ps[:, p, F:], ALU.mult).then_inc(hid_done, 1)

            def copy_hidden(t, p):
                dve.wait_ge(hid_turned, t + 1)
                if live(t - 2, N):
                    dve.wait_ge(down_done, t - 1)
                nc.vector.tensor_copy(hid_t[:, p], ht_ps[:, p, 0:F].rearrange("k (c t) -> k c t", c=FC))\
                    .then_inc(hid_copied, 1)

            def copy_y(t, p):
                dve.wait_ge(down_done, t + 1)
                if live(t - 2, N):
                    dve.wait_ge(y_written[p], landed(t - 2, p))
                nc.vector.tensor_copy(y[:, p], down_ps[:, p]).then_inc(y_done, 1)

            def step(i, p):
                if live(i, N):
                    hidden(i, p)
                if live(i - 1, N):
                    copy_y(i - 1, 1 - p)
                if live(i, N):
                    copy_hidden(i, p)

            run_steps(dve, step, 0, 4, N - 1, N)

        @block.scalar
        def _(act):
            def copy_xt(t, p):
                act.wait_ge(turned, t + 1)
                if live(t - 2, N):
                    act.wait_ge(gu_done, t - 1)
                nc.scalar.activation(xt[:, p], turn_ps[:, :].rearrange("k (c t) -> k c t", c=DC), ACT.Copy)\
                    .then_inc(xt_copied, 1)

            def silu(t, p):
                act.wait_ge(gu_done, t + 1)
                if live(t - 2, N):
                    act.wait_ge(hid_done, t - 1)
                nc.scalar.activation(gate[:, p], gu_ps[:, p, 0:F], ACT.Silu).then_inc(gated, 1)

            def step(i, p):
                if live(i, N):
                    silu(i, p)
                if live(i + 1, N):
                    copy_xt(i + 1, 1 - p)

            run_steps(act, step, -1, 3, N - 2, N - 1)

        @block.tensor
        def _(pe):
            def owner(t):
                return pe.value_load(keep["owner"][0:1, column(t)], min_val=0, max_val=E - 1)

            def turn(t, p):
                pe.wait_ge(x_loaded[p], landed(t, p, 16, RING))
                if live(t - 1, N):
                    pe.wait_ge(xt_copied, t)
                for c in range(DC):
                    last = nc.tensor.transpose(turn_ps[:, c * P:(c + 1) * P], x[:, p, c * P:(c + 1) * P],
                                               keep["ident"][:, :])
                last.then_inc(turned, 1)

            def gate_up(t, p):
                e = owner(t)
                pe.wait_ge(xt_copied, t + 1)
                if live(t - 2, N):
                    pe.wait_ge(hid_done, t - 1)
                for c in range(DC):
                    last = nc.tensor.matmul(gu_ps[:, p], xt[:, p, c],
                                            keep["gate_up"][:, bass.ds(e * (DC * 2 * F) + c * 2 * F, 2 * F)],
                                            start=(c == 0), stop=(c == DC - 1))
                last.then_inc(gu_done, 1)

            def turn_hidden(t, p):
                pe.wait_ge(hid_done, t + 1)
                if live(t - 2, N):
                    pe.wait_ge(hid_copied, t - 1)
                for c in range(FC):
                    last = nc.tensor.transpose(ht_ps[:, p, c * P:(c + 1) * P], hid[:, p, c * P:(c + 1) * P],
                                               keep["ident"][:, :])
                last.then_inc(hid_turned, 1)

            def down(t, p):
                e = owner(t)
                pe.wait_ge(hid_copied, t + 1)
                if live(t - 2, N):
                    pe.wait_ge(y_done, t - 1)
                for c in range(FC):
                    last = nc.tensor.matmul(down_ps[:, p], hid_t[:, p, c],
                                            keep["down_flat"][:, bass.ds(e * (FC * D) + c * D, D)],
                                            start=(c == 0), stop=(c == FC - 1))
                last.then_inc(down_done, 1)

            def step(i, p):
                if live(i, N):
                    gate_up(i, p % 2)
                if live(i + 1, N):
                    turn(i + 1, (p + 1) % RING)
                if live(i - 1, N):
                    down(i - 1, (p + 1) % 2)
                if live(i, N):
                    turn_hidden(i, p % 2)

            run_steps(pe, step, -1, 4, N - 3, N, RING)


def combine(nc, acc_dram, y_dram, out, keep):
    RING = 4
    y_rows = y_dram.rearrange("i p d -> (i p) d")
    with ExitStack() as ctx:
        sb = lambda name, shape, dt: ctx.enter_context(nc.sbuf_tensor(name, shape, dt))
        sem = lambda name: ctx.enter_context(nc.semaphore(name))
        acc = sb("c_acc", [P, RING, D], F32)
        y = sb("c_y", [P, RING, TOP, D], F32)
        acc_loaded = [sem(f"c_acc_loaded{k}") for k in range(RING)]
        gathered = [sem(f"c_gathered{k}") for k in range(RING)]
        summed = sem("c_summed")
        out_done = sem("c_out_done")
        out_written = [sem(f"c_out_written{k}") for k in range(RING)]

        block = ctx.enter_context(nc.Block())

        @block.sync
        def _(sp):
            def load(t, p):
                if live(t - RING):
                    sp.wait_ge(out_written[p], landed(t - RING, p, 16, RING))
                sp.dma_start(acc[:, p], at(acc_dram, t)).then_inc(acc_loaded[p], 16)

            def write(t, p):
                sp.wait_ge(out_done, t + 1)
                sp.dma_start(at(out, t), acc[:, p]).then_inc(out_written[p], 16)

            def step(b, p):
                if live(b + 3):
                    load(b + 3, (p + 3) % RING)
                if live(b):
                    write(b, p)

            run_steps(sp, step, -3, 1, 29, 31, RING)
            drain_ring(sp, out_written, B)

        @block.gpsimd
        def _(pool):
            for t in range(B):
                if live(t - RING):
                    pool.wait_ge(out_done, t - RING + 1)
                for k in range(TOP):
                    nc.gpsimd.indirect_dma_start(
                        out=y[:, t % RING, k], out_offset=None, in_=y_rows,
                        in_offset=bass.IndirectOffsetOnAxis(ap=keep["place"][:, t, k:k + 1], axis=0))\
                        .then_inc(gathered[t % RING], 16)

        @block.vector
        def _(dve):
            def step(b, p):
                dve.wait_ge(gathered[p], landed(b, p, 32, RING))
                nc.vector.tensor_tensor(y[:, p, 0], y[:, p, 0], y[:, p, 1], ALU.add).then_inc(summed, 1)
                dve.wait_ge(acc_loaded[p], landed(b, p, 16, RING))
                dve.wait_ge(summed, b + 1)
                nc.vector.tensor_tensor(acc[:, p], acc[:, p], y[:, p, 0], ALU.add).then_inc(out_done, 1)

            run_steps(dve, step, 0, 0, 32, 31, RING)


def program(nc, x, ctx_2048, itok_B_779_1933, router_w, gate_up_w, down_w, shared_gate_w, shared_up_w,
            shared_down_w, out):
    scr = lambda name, shape: nc.dram_tensor(name, shape, F32, kind="Internal").ap()
    x2_dram = scr("x2_dram", [B, P, D])
    acc_dram = scr("acc_dram", [B, P, D])
    y_dram = scr("y_dram", [TILES, P, D])
    with ExitStack() as ctx:
        sb = lambda name, shape, dt: ctx.enter_context(nc.sbuf_tensor(name, shape, dt))
        gate_up = sb("gate_up", [P, E * DC * 2 * F], F32)
        shared_gu = sb("shared_gu", [P, DC, 2 * F], F32)
        shared_down = sb("shared_down", [P, FC, D], F32)
        router = sb("router", [P, DC, E], F32)
        keep = {
            "rows_dram": scr("rows_dram", [TILES * P, D]),
            "ident": sb("ident", [P, P], F32),
            "router": router,
            "shared_gu": shared_gu,
            "shared_down": shared_down,
            "gate_up": gate_up,
            "weights_loaded": ctx.enter_context(nc.semaphore("weights_loaded")),
        }
        gu_e = gate_up[:, :].rearrange("p (e c n) -> p e c n", e=E, c=DC)
        keep["weight_loads"] = [(gu_e[:, e], gate_up_w[e].rearrange("(c p) n -> p c n", p=P)) for e in range(E)]
        keep["weight_loads"] += [
            (shared_gu[:, :, 0:F], shared_gate_w.rearrange("(c p) n -> p c n", p=P)),
            (shared_gu[:, :, F:], shared_up_w.rearrange("(c p) n -> p c n", p=P)),
            (shared_down[:, :, :], shared_down_w.rearrange("(c p) n -> p c n", p=P)),
            (router[:, :, :], router_w.rearrange("(c p) n -> p c n", p=P))]
        keep["weights_count"] = 16 * len(keep["weight_loads"])
        attention(nc, x, ctx_2048, itok_B_779_1933, x2_dram, keep)
        keep["top_val"] = sb("top_val_all", [P, B, TOP], F32)
        keep["top_idx"] = sb("top_idx_all", [P, B, TOP], F32)
        keep["prob"] = sb("prob_all", [P, B, TOP], F32)
        keep["place"] = sb("place_all", [P, B, TOP], U32)
        keep["owner"] = sb("owner_all", [P, TILES], I32)
        down_flat = sb("down", [P, E * FC * D], F32)
        keep["down_flat"] = down_flat
        keep["down"] = down_flat[:, :].rearrange("p (e c n) -> p e c n", e=E, c=FC)
        with nc.sbuf_tensor("xn_all", [P, B, D], F32) as xn:
            keep["xn"] = xn
            route(nc, x2_dram, down_w, keep)
            dispatch(nc, x2_dram, acc_dram, keep)
        experts(nc, y_dram, keep)
        combine(nc, acc_dram, y_dram, out, keep)


_INS = ["x", "ctx_2048", "itok_B_779_1933", "L0_ffn_router_w", "L0_ffn_gate_up_w", "L0_ffn_down_w",
        "L0_ffn_shared_gate_w", "L0_ffn_shared_up_w", "L0_ffn_shared_down_w"]
_OUTS = [((B, ROWS, L), "float32")]


def kernel(**inputs):
    import numpy as _np
    import concourse.bacc as _bacc
    from concourse import mybir as _mybir
    from concourse.bass_utils import run_bass_kernel_spmd as _run

    nc = _bacc.Bacc("TRN2", target_bir_lowering=False, num_devices=1)
    arrays, args = {}, []
    for name in _INS:
        a = _np.ascontiguousarray(inputs[name])
        arrays[f"in_{name}_dram"] = a
        args.append(nc.dram_tensor(f"in_{name}_dram", a.shape, _mybir.dt.from_np(a.dtype), kind="ExternalInput").ap())
    for i, (shape, dtype) in enumerate(_OUTS):
        dt = _mybir.dt.from_np(_np.dtype(dtype))
        args.append(nc.dram_tensor(f"out_{i}_dram", shape, dt, kind="ExternalOutput").ap())
    program(nc, *args)
    r = _run(nc, [arrays], core_ids=[0])
    got = tuple(r.results[0][f"out_{i}_dram"] for i in range(len(_OUTS)))
    return got[0]
```

```python
from contextlib import ExitStack

import numpy as np

import concourse.bass as bass
from concourse import mybir

F32 = mybir.dt.float32
BF16 = mybir.dt.bfloat16
I32 = mybir.dt.int32
U32 = mybir.dt.uint32
ALU = mybir.AluOpType
ACT = mybir.ActivationFunctionType
AX = mybir.AxisListType

P = 128
B, ROWS, L = 32, 128, 512
H, DH = 8, 16
SETS, HS = 2, 4
KT = L // P
GROUPS = SETS * KT
UNITS = GROUPS * HS
PAIRS = H * KT // 2
PARTS = 3
Q_PART = (0, 1, 2, 0, 1, 0)
K_PART = (2, 1, 0, 1, 0, 0)
Q_SLOT = (0, 1, 2)
K_SLOT = (5, 4, 3)
STACK = len(Q_PART) * DH
SLOT = 32
LN_EPS = 1e-5
SCALE = 1.0 / (64 ** 0.5 * float(np.log(20)))

T = B * ROWS
D = L
E, F = 8, 256
TOP = 2
DC = D // P
FC = F // P
TILES = T * TOP // P + E - 1


def live(n, count=B):
    return 0 <= n < count if isinstance(n, int) else True


def run_steps(eng, step, first, lo, hi, last, ring=2):
    for b in range(first, lo):
        step(b, b % ring)
    with eng.Fori(0, (hi - lo) // ring) as i:
        b = eng.snap(i * ring + lo)
        for k in range(ring):
            step(b + k, (lo + k) % ring)
    for b in range(hi, last + 1):
        step(b, b % ring)


def at(dram, b):
    if isinstance(b, int):
        return dram[b]
    n = "abcdef"[:len(dram.shape) - 1]
    return dram[bass.ds(b, 1)].rearrange(f"z {' '.join(n)} -> (z {n[0]}) {' '.join(n[1:])}")


def wait_apart(nc, dve, semaphore, value, mark, slot=1):
    dve.wait_ge(semaphore, value)
    nc.vector.tensor_copy(mark[0:1, slot:slot + 1], mark[0:1, 0:1])


def landed(t, k, inc=16, ring=2):
    return inc // ring * t + (inc - inc // ring * k)


def drain_ring(eng, sems, count, inc=16):
    for k, s in enumerate(sems):
        eng.wait_ge(s, inc * len(range(k, count, len(sems))))


def count_of(eng, value):
    return value if isinstance(value, int) else eng.snap(value)


def attention(nc, x, ctx_in, lengths, x2_dram, keep):
    scr = lambda name, shape, dt: nc.dram_tensor(name, shape, dt, kind="Internal").ap()
    split_dram = scr("split_dram", [B, 2 * PARTS, DH, H, L], BF16)
    o_dram = scr("o_dram", [B, H, SLOT, L], F32)
    rden_dram = scr("rden_dram", [B, H, L], F32)

    with ExitStack() as ctx:
        sb = lambda name, shape, dt: ctx.enter_context(nc.sbuf_tensor(name, shape, dt))
        ps = lambda name, shape, dt: ctx.enter_context(nc.psum_tensor(name, shape, dt))
        sem = lambda name: ctx.enter_context(nc.semaphore(name))

        x_in = sb("x_in", [P, 2, L], F32)
        ctx_sb = sb("ctx_sb", [P, 2, L], F32)
        q_norm = sb("q_norm", [P, 2, L], F32)
        split_sb = sb("split_sb", [P, 2, 2 * PARTS, L], BF16)
        q_rest = sb("q_rest", [P, L], F32)
        k_rest = sb("k_rest", [P, L], F32)
        stack = sb("stack", [P, 2, 2, H, L], BF16)
        v_t = sb("v_t", [P, 2, KT, H, SLOT], F32)
        probs = sb("probs", [P, 2, HS, L], F32)
        o_sb = sb("o_sb", [P, 2, SETS, L], F32)
        den = sb("den", [P, 2, H * L // P], F32)
        rden = sb("rden", [P, 2, H * L // P], F32)
        num = sb("num", [P, 2, L], F32)
        rden_rows = sb("rden_rows", [P, 2, L], F32)
        x_again = sb("x_again", [P, 2, L], F32)
        neg_max = sb("neg_max", [P, 2, H * KT], F32)
        nm_split = sb("nm_split", [P, SETS, PARTS, HS * KT], BF16)
        nm_rest = sb("nm_rest", [P, HS * KT], F32)
        nm_rows = sb("nm_rows", [PARTS * HS * KT, SETS, P], BF16)
        ident_bf = sb("ident_bf", [P, P], BF16)
        stats = sb("stats", [P, 6], F32)
        moments = sb("moments", [P, 2], F32)
        mark = sb("mark", [1, 2], F32)
        var_eps = sb("var_eps", [P, 1], F32)
        power = sb("power", [P, 1], F32)
        rstd = sb("rstd", [P, 1], F32)
        q_scale = sb("q_scale", [P, 1], F32)
        len_i = sb("len_i", [P, B], I32)
        len_f = sb("len_f", [P, B], F32)
        len_ln = sb("len_ln", [P, B], F32)
        len_scale = sb("len_scale", [P, B], F32)
        zeros = sb("zeros", [P, TILES * D // B], F32)
        ident = keep["ident"]

        smax_ps = ps("smax_ps", [P, 2, 2, L], F32)
        st_ps = ps("st_ps", [P, 2, L], F32)
        o_ps = ps("o_ps", [P, L], F32)
        turn_ps = ps("turn_ps", [P, L], F32)

        consts = sem("consts")
        shift_ones = sem("shift_ones")
        len_loaded = sem("len_loaded")
        len_ready = sem("len_ready")
        x_loaded = [sem(f"x_loaded{k}") for k in range(2)]
        ctx_loaded = [sem(f"ctx_loaded{k}") for k in range(2)]
        norm_steps = sem("norm_steps")
        rstd_ready = sem("rstd_ready")
        q_normed = sem("q_normed")
        hi_ready = sem("hi_ready")
        split_steps = sem("split_steps")
        k_split_done = sem("k_split_done")
        q_split_done = sem("q_split_done")
        split_written = sem("split_written")
        stack_loaded = [sem(f"stack_loaded{s}") for s in range(SETS)]
        nm_loaded = [sem(f"nm_loaded{s}") for s in range(SETS)]
        v_turned = sem("v_turned")
        v_copied = sem("v_copied")
        smax_done = sem("smax_done")
        max_done = sem("max_done")
        nm_first = sem("nm_first")
        nm_steps = sem("nm_steps")
        nm_split_done = sem("nm_split_done")
        nm_turned = sem("nm_turned")
        nm_copied = sem("nm_copied")
        st_done = sem("st_done")
        exp_done = sem("exp_done")
        pv_done = sem("pv_done")
        o_copied = sem("o_copied")
        o_written = sem("o_written")
        den_loaded = sem("den_loaded")
        rden_ready = sem("rden_ready")
        rden_written = sem("rden_written")
        parts_loaded = [sem(f"parts_loaded{k}") for k in range(2)]
        mixed = sem("mixed")
        x2_ready = sem("x2_ready")
        x2_written = [sem(f"x2_written{k}") for k in range(2)]
        zeros_written = sem("zeros_written")

        block = ctx.enter_context(nc.Block())

        @block.sync
        def _(sp):
            sp.dma_start(len_i[:, :], bass.AP(lengths.tensor, 0, [[0, P], [1, B]])).then_inc(len_loaded, 16)

            def load(t, p):
                if live(t - 2):
                    sp.wait_ge(q_normed, t - 1)
                sp.dma_start(x_in[:, p], at(x, t).rearrange("(h d) f -> d h f", h=H)).then_inc(x_loaded[p], 16)
                if live(t - 2):
                    sp.wait_ge(v_turned, t - 1)
                    sp.wait_ge(k_split_done, t - 1)
                sp.dma_start(ctx_sb[:, p], at(ctx_in, t).rearrange("(h d) f -> d h f", h=H))\
                    .then_inc(ctx_loaded[p], 16)

            def write_split(t, p):
                sp.wait_ge(k_split_done, t + 1)
                sp.wait_ge(q_split_done, t + 1)
                sp.dma_start(at(split_dram, t).rearrange("j d h f -> (d h) j f"), split_sb[:, p])\
                    .then_inc(split_written, 16)

            def load_stack(t, p, s):
                written = count_of(sp, 16 * t + 16)
                if live(t - 2):
                    sp.wait_ge(st_done, UNITS * (t - 2) + UNITS // 2 * (s + 1))
                sp.wait_ge(split_written, written)
                row = 0
                for run in (3, 2, 1):
                    src = at(split_dram, t)[:, :, HS * s:HS * (s + 1), :]\
                        .rearrange("(a t) d h f -> t d a h f", t=run)
                    sp.dma_start(stack[row:row + run * DH, p, :, HS * s:HS * (s + 1), :],
                                 src[:, :, ::2 * PARTS // run - 1]).then_inc(stack_loaded[s], 16)
                    row += run * DH

            def load_shift(t, p, s):
                sp.wait_ge(nm_copied, 2 * t + s + 1)
                sp.dma_start(stack[STACK:STACK + PARTS, p, 0, HS * s:HS * (s + 1), :], nm_rows[:, s, :])\
                    .then_inc(nm_loaded[s], 16)

            def write_o(t, p):
                sp.wait_ge(o_copied, 2 * t + 2)
                sp.dma_start(at(o_dram, t).rearrange("(s j) r f -> (j r) s f", s=SETS), o_sb[:, p])\
                    .then_inc(o_written, 16)

            def load_den(t, p):
                sp.wait_ge(o_written, 16 * t + 16)
                sp.dma_start(den[:, p], at(o_dram, t)[:, DH, :].rearrange("h (c w) -> h c w", c=P // H))\
                    .then_inc(den_loaded, 16)

            def write_rden(t, p):
                sp.wait_ge(rden_ready, t + 1)
                sp.dma_start(at(rden_dram, t), rden[:, p]).then_inc(rden_written, 16)

            def load_parts(t, p):
                if live(t - 2):
                    sp.wait_ge(x2_written[p], landed(t - 2, p))
                sp.dma_start(num[:, p], at(o_dram, t)[:, 0:DH, :]).then_inc(parts_loaded[p], 16)
                sp.dma_start(x_again[:, p], at(x, t)).then_inc(parts_loaded[p], 16)
                sp.wait_ge(rden_written, 16 * t + 16)
                sp.dma_start(rden_rows[:, p], at(rden_dram, t).rearrange("h (o f) -> h o f", o=1)
                             .broadcast_to([H, DH, L])).then_inc(parts_loaded[p], 16)

            def write_x2(t, p):
                sp.wait_ge(x2_ready, t + 1)
                sp.dma_start(at(x2_dram, t), x_again[:, p]).then_inc(x2_written[p], 16)

            def clear_rows(t):
                if isinstance(t, int) and t == 0:
                    sp.wait_ge(consts, 6)
                sp.dma_start(at(keep["rows_dram"].rearrange("(b r) d -> b r d", b=B), t), zeros[:, :])\
                    .then_inc(zeros_written, 16)

            loads = {b: [] for b in (0, 1, 2, 3, 4, 29, 30, 31, 32)}
            for n, load_of in enumerate(keep["weight_loads"]):
                loads[list(loads)[n % len(loads)]].append(load_of)

            def step(b, p):
                if live(b + 1):
                    load_stack(b + 1, 1 - p, 1)
                if live(b - 2):
                    write_rden(b - 2, p)
                if live(b - 1):
                    write_o(b - 1, 1 - p)
                if live(b):
                    load_shift(b, p, 1)
                if live(b - 2):
                    load_parts(b - 2, p)
                if live(b - 3):
                    write_x2(b - 3, 1 - p)
                if live(b - 1):
                    load_den(b - 1, 1 - p)
                if live(b + 3):
                    load(b + 3, 1 - p)
                if live(b):
                    clear_rows(b)
                if live(b + 2):
                    write_split(b + 2, p)
                    load_stack(b + 2, p, 0)
                if live(b + 1):
                    load_shift(b + 1, 1 - p, 0)
                for dst, src in loads.get(b, ()) if isinstance(b, int) else ():
                    sp.dma_start(dst, src).then_inc(keep["weights_loaded"], 16)

            run_steps(sp, step, -3, 5, 29, 34)
            drain_ring(sp, x2_written, B)
            sp.wait_ge(zeros_written, 16 * B)

        @block.gpsimd
        def _(pool):
            nc.gpsimd.memset(ident[:, :], 0.0).then_inc(consts, 1)
            nc.gpsimd.memset(v_t[:, :], 0.0).then_inc(consts, 1)
            nc.gpsimd.memset(zeros[:, :], 0.0).then_inc(consts, 1)
            nc.gpsimd.memset(power[:, :], -0.5).then_inc(consts, 1)
            pool.wait_ge(consts, 4)
            nc.gpsimd.affine_select(out=ident[:, :], in_=ident[:, :], compare_op=ALU.not_equal, fill=1.0,
                                    base=0, pattern=[[-1, P]], channel_multiplier=1).then_inc(consts, 1)
            nc.gpsimd.memset(v_t[:, :, :, :, DH:DH + 1], 1.0).then_inc(consts, 1)

            def split(t, p, src, slot, rest, hi_count, done):
                n = 4 * t + (0 if done is k_split_done else 2)
                first, second, third = (split_sb[:, p, j] for j in slot)
                pool.wait_ge(hi_ready, hi_count)
                nc.gpsimd.tensor_tensor(second, src[:, p], first, ALU.subtract).then_inc(split_steps, 1)
                if live(t - 1):
                    pool.wait_ge(done, t)
                nc.gpsimd.tensor_tensor(rest[:, :], src[:, p], first, ALU.subtract).then_inc(split_steps, 1)
                pool.wait_ge(split_steps, n + 2)
                nc.gpsimd.tensor_tensor(third, rest[:, :], second, ALU.subtract).then_inc(done, 1)

            def split_max(t, p, s):
                n = 2 * t + s
                value = neg_max[:, p, HS * KT * s:HS * KT * (s + 1)]
                pool.wait_ge(nm_first, n + 1)
                nc.gpsimd.tensor_tensor(nm_split[:, s, 1], value, nm_split[:, s, 0], ALU.subtract)\
                    .then_inc(nm_steps, 1)
                if not (isinstance(n, int) and n == 0):
                    pool.wait_ge(nm_split_done, n)
                nc.gpsimd.tensor_tensor(nm_rest[:, :], value, nm_split[:, s, 0], ALU.subtract)\
                    .then_inc(nm_steps, 1)
                pool.wait_ge(nm_steps, 2 * n + 2)
                nc.gpsimd.tensor_tensor(nm_split[:, s, 2], nm_rest[:, :], nm_split[:, s, 1], ALU.subtract)\
                    .then_inc(nm_split_done, 1)

            def residual(t, p):
                pool.wait_ge(parts_loaded[p], landed(t, p, 48))
                nc.gpsimd.tensor_tensor(num[:, p], num[:, p], rden_rows[:, p], ALU.mult).then_inc(mixed, 1)
                pool.wait_ge(mixed, t + 1)
                nc.gpsimd.tensor_tensor(x_again[:, p], num[:, p], x_again[:, p], ALU.add).then_inc(x2_ready, 1)

            def step(b, p):
                if live(b):
                    split_max(b, p, 1)
                if live(b + 2):
                    pool.wait_ge(norm_steps, 4 * (b + 2) + 3)
                    nc.gpsimd.tensor_tensor(rstd[:, :], var_eps[:, :], power[:, :], ALU.pow).then_inc(rstd_ready, 1)
                    split(b + 2, p, ctx_sb, K_SLOT, k_rest, 2 * (b + 2) + 1, k_split_done)
                    split(b + 2, p, q_norm, Q_SLOT, q_rest, 2 * (b + 2) + 2, q_split_done)
                if live(b + 1):
                    split_max(b + 1, 1 - p, 0)
                if live(b - 2):
                    residual(b - 2, p)

            run_steps(pool, step, -2, 2, 30, 33)

        @block.vector
        def _(dve):
            nc.vector.memset(mark[:, :], 0.0)
            dve.wait_ge(consts, 6)
            nc.vector.tensor_copy(ident_bf[:, :], ident[:, :]).then_inc(shift_ones, 1)
            dve.wait_ge(len_loaded, 16)
            nc.vector.tensor_copy(len_f[:, :], len_i[:, :]).then_inc(len_ready, 1)
            dve.wait_ge(len_ready, 2)
            nc.vector.tensor_scalar(len_scale[:, :], len_ln[:, :], SCALE, None, ALU.mult).then_inc(len_ready, 1)
            dve.wait_ge(len_ready, 3)

            def k_first(t, p):
                dve.wait_ge(ctx_loaded[p], landed(t, p))
                if live(t - 2):
                    dve.wait_ge(split_written, 16 * (t - 1))
                nc.vector.tensor_copy(split_sb[:, p, K_SLOT[0]], ctx_sb[:, p]).then_inc(hi_ready, 1)

            def norm_stats(t, p):
                dve.wait_ge(x_loaded[p], landed(t, p))
                nc.vector.bn_stats(stats[:, :], x_in[:, p]).then_inc(norm_steps, 1)

            def norm_moments(t, p):
                wait_apart(nc, dve, norm_steps, 4 * t + 1, mark)
                nc.vector.bn_aggr(moments[:, :], stats[:, :]).then_inc(norm_steps, 1)

            def norm_var(t, p):
                dve.wait_ge(norm_steps, 4 * t + 2)
                nc.vector.tensor_scalar(var_eps[:, :], moments[:, 1:2], LN_EPS, None, ALU.add)\
                    .then_inc(norm_steps, 1)

            def norm_scale(t, p):
                dve.wait_ge(rstd_ready, t + 1)
                col = len_scale[:, t:t + 1] if isinstance(t, int) else len_scale[:, bass.ds(t, 1)]
                nc.vector.tensor_tensor(q_scale[:, :], rstd[:, :], col, ALU.mult).then_inc(norm_steps, 1)

            def norm_apply(t, p):
                dve.wait_ge(norm_steps, 4 * t + 4)
                if live(t - 2):
                    dve.wait_ge(q_split_done, t - 1)
                nc.vector.tensor_scalar(q_norm[:, p], x_in[:, p], moments[:, 0:1], q_scale[:, :],
                                        ALU.subtract, ALU.mult).then_inc(q_normed, 1)

            def q_first(t, p):
                dve.wait_ge(q_normed, t + 1)
                nc.vector.tensor_copy(split_sb[:, p, Q_SLOT[0]], q_norm[:, p]).then_inc(hi_ready, 1)

            def invert(t, p):
                dve.wait_ge(den_loaded, 16 * t + 16)
                if live(t - 2):
                    dve.wait_ge(rden_written, 16 * (t - 1))
                nc.vector.reciprocal(rden[:, p], den[:, p]).then_inc(rden_ready, 1)

            def row_max(t, p, i):
                dve.wait_ge(smax_done, PAIRS * t + i + 1)
                nc.vector.tensor_reduce(neg_max[:, p, 2 * i:2 * i + 2], smax_ps[:, i % 2], AX.X, ALU.max,
                                        negate=True).then_inc(max_done, 1)

            def max_first(t, p, s):
                if not (isinstance(t, int) and t == 0):
                    dve.wait_ge(nm_turned, 2 * t + s - 1)
                dve.wait_ge(max_done, PAIRS * t + PAIRS // 2 * (s + 1))
                nc.vector.tensor_copy(nm_split[:, s, 0], neg_max[:, p, HS * KT * s:HS * KT * (s + 1)])\
                    .then_inc(nm_first, 1)

            between = {0: (k_first, norm_stats), 1: (norm_moments, norm_var), 3: (norm_scale, norm_apply),
                       4: (q_first,)}

            def step(b, p):
                if isinstance(b, int) and b == -1:
                    nc.vector.memset(stack[STACK:STACK + PARTS, :, 1, :, :], 1.0).then_inc(shift_ones, 1)
                for i in range(PAIRS):
                    if live(b + 1):
                        row_max(b + 1, 1 - p, i)
                    if live(b + 1) and i % (PAIRS // 2) == PAIRS // 2 - 1:
                        max_first(b + 1, 1 - p, i // (PAIRS // 2))
                    for part in between.get(i, ()) if live(b + 2) else ():
                        part(b + 2, p)
                    if i == 12 and live(b - 1):
                        invert(b - 1, 1 - p)

            run_steps(dve, step, -2, 3, 29, 32)

        @block.scalar
        def _(act):
            act.wait_ge(len_ready, 1)
            nc.scalar.activation(len_ln[:, :], len_f[:, :], ACT.Ln).then_inc(len_ready, 1)

            def copy_v(t, p):
                act.wait_ge(v_turned, t + 1)
                if live(t - 2):
                    act.wait_ge(pv_done, GROUPS * (t - 1))
                else:
                    act.wait_ge(consts, 6)
                nc.scalar.activation(v_t[:, p, :, :, 0:DH], turn_ps[:, :].rearrange(
                    "k (t d h) -> k t h d", t=KT, h=H), ACT.Copy).then_inc(v_copied, 1)

            def copy_nm(t, s):
                act.wait_ge(nm_turned, 2 * t + s + 1)
                if live(t - 1):
                    act.wait_ge(nm_loaded[s], 16 * t)
                nc.scalar.activation(nm_rows[:, s], turn_ps[0:PARTS * HS * KT, 0:P], ACT.Copy)\
                    .then_inc(nm_copied, 1)

            def exponentials(t, s, g, j):
                u = UNITS * t + HS * (KT * s + g) + j
                act.wait_ge(st_done, u + 1)
                if j == 0 and not (isinstance(t, int) and t == 0 and s == 0 and g < 2):
                    act.wait_ge(pv_done, GROUPS * t + KT * s + g - 1)
                nc.scalar.activation(probs[:, g % 2, j], st_ps[:, j % 2], ACT.Exp).then_inc(exp_done, 1)

            def copy_o(t, p, s):
                act.wait_ge(pv_done, GROUPS * t + KT * (s + 1))
                if live(t - 2):
                    act.wait_ge(o_written, 16 * (t - 1))
                nc.scalar.activation(o_sb[:, p, s], o_ps[:, :], ACT.Copy).then_inc(o_copied, 1)

            def step(b, p):
                for s in range(SETS):
                    for g in range(KT):
                        for j in range(HS):
                            if live(b):
                                exponentials(b, s, g, j)
                            if g == 0 and j == 3:
                                if s == 0 and live(b - 1):
                                    copy_o(b - 1, 1 - p, 1)
                                if s == 1 and live(b):
                                    copy_o(b, p, 0)
                            if g == 1 and j == 1:
                                if s == 0 and live(b):
                                    copy_nm(b, 1)
                                if s == 1 and live(b + 1):
                                    copy_nm(b + 1, 0)
                            if g == 3 and j == 1 and s == 0 and live(b + 1):
                                copy_v(b + 1, 1 - p)

            run_steps(act, step, -1, 3, 31, 32)

        @block.tensor
        def _(pe):
            pe.wait_ge(consts, 6)

            def turn_free(n_v, n_nm):
                for s, n in ((v_copied, n_v), (nm_copied, n_nm)):
                    if not (isinstance(n, int) and n <= 0):
                        pe.wait_ge(s, n)

            def turn_v(t, p):
                turn_free(t, 2 * t)
                pe.wait_ge(ctx_loaded[p], landed(t, p))
                for k in range(KT):
                    last = nc.tensor.transpose(turn_ps[:, k * P:(k + 1) * P], ctx_sb[:, p, k * P:(k + 1) * P],
                                               ident[:, :])
                last.then_inc(v_turned, 1)

            def turn_nm(t, s):
                if isinstance(t, int) and t == 0 and s == 0:
                    pe.wait_ge(shift_ones, 2)
                pe.wait_ge(nm_split_done, 2 * t + s + 1)
                turn_free(t + 1, 2 * t + s)
                nc.tensor.matmul(turn_ps[0:PARTS * HS * KT, 0:P], nm_split[:, s].rearrange("p a c -> p (a c)"),
                                 ident_bf[:, :], start=True, stop=True).then_inc(nm_turned, 1)

            def scores_for_max(t, p, h, pair):
                i = 2 * h + pair
                if h % HS == 0 and pair == 0:
                    pe.wait_ge(stack_loaded[h // HS], 48 * (t + 1))
                if not (isinstance(t, int) and t == 0 and i < 2):
                    pe.wait_ge(max_done, PAIRS * t + i - 1)
                for c in range(2):
                    q0 = (2 * pair + c) * P
                    last = nc.tensor.matmul(smax_ps[:, i % 2, c], stack[0:STACK, p, 0, h, q0:q0 + P],
                                            stack[0:STACK, p, 1, h, :], start=True, stop=True)
                last.then_inc(smax_done, 1)

            def scores(t, p, s, g, j):
                u = UNITS * t + HS * (KT * s + g) + j
                h = HS * s + j
                if isinstance(u, int) and u == 0:
                    pe.wait_ge(shift_ones, 2)
                if g == 0 and j == 0:
                    pe.wait_ge(nm_loaded[s], 16 * (t + 1))
                if not (isinstance(u, int) and u < 2):
                    pe.wait_ge(exp_done, u - 1)
                nc.tensor.matmul(st_ps[:, j % 2], stack[0:STACK + PARTS, p, 1, h, g * P:(g + 1) * P],
                                 stack[0:STACK + PARTS, p, 0, h, :], start=True, stop=True).then_inc(st_done, 1)

            def attend(t, p, s, g, half):
                n = GROUPS * t + KT * s + g
                if half == 0:
                    if g == 0:
                        pe.wait_ge(v_copied, t + 1)
                        if not (isinstance(t, int) and t == 0 and s == 0):
                            pe.wait_ge(o_copied, 2 * t + s)
                    pe.wait_ge(exp_done, HS * n + HS)
                cols = slice(half * L // 2, (half + 1) * L // 2)
                for j in range(HS):
                    last = nc.tensor.matmul(o_ps[SLOT * j:SLOT * (j + 1), cols], v_t[:, p, g, HS * s + j, :],
                                            probs[:, g % 2, j, cols], start=(g == 0 and half == 0),
                                            stop=(g == KT - 1 and half == 1),
                                            tile_position=(0, SLOT * j))
                if half == 1:
                    last.then_inc(pv_done, 1)

            def step(b, p):
                for s in range(SETS):
                    for g in range(KT):
                        h = HS * s + g
                        for j in range(HS):
                            if live(b):
                                scores(b, p, s, g, j)
                            if j % 2 == 0:
                                if live(b + 1):
                                    scores_for_max(b + 1, 1 - p, h, j // 2)
                            elif h > 0:
                                if live(b):
                                    attend(b, p, (h - 1) // KT, (h - 1) % KT, j // 2)
                            elif live(b - 1):
                                attend(b - 1, 1 - p, 1, KT - 1, j // 2)
                        if g == 0 and s == 0 and live(b):
                            turn_nm(b, 1)
                        if g == 0 and s == 1 and live(b + 1):
                            turn_nm(b + 1, 0)
                        if g == 2 and s == 0 and live(b + 1):
                            turn_v(b + 1, 1 - p)

            run_steps(pe, step, -1, 1, 31, 32)


def column(t):
    return slice(t, t + 1) if isinstance(t, int) else bass.ds(t, 1)


def route(nc, x2_dram, down_w, keep):
    RING = 4
    with ExitStack() as ctx:
        sb = lambda name, shape, dt: ctx.enter_context(nc.sbuf_tensor(name, shape, dt))
        ps = lambda name, shape, dt: ctx.enter_context(nc.psum_tensor(name, shape, dt))
        sem = lambda name: ctx.enter_context(nc.semaphore(name))

        x2_in = sb("r_x2_in", [P, RING, D], F32)
        xn = sb("r_xn", [P, 2, D], F32)
        xt = sb("r_xt", [P, 2, DC, P], F32)
        stats = sb("r_stats", [P, 6], F32)
        moments = sb("r_moments", [P, 2], F32)
        mark = sb("r_mark", [1, 4], F32)
        var_eps = sb("r_var_eps", [P, 1], F32)
        power = sb("r_power", [P, 1], F32)
        rstd = sb("r_rstd", [P, 1], F32)
        logits = sb("r_logits", [P, 2, E], F32)
        top_val = sb("r_top_val", [P, 2, 8], F32)
        top_idx = sb("r_top_idx", [P, 2, 8], U32)
        turn_ps = ps("r_turn_ps", [P, 2, D], F32)
        logit_ps = ps("r_logit_ps", [P, 2, 512], F32)

        x2_loaded = [sem(f"x2_loaded{k}") for k in range(RING)]
        down_loaded = sem("down_loaded")
        steps = sem("r_norm_steps")
        power_ready = sem("r_power_ready")
        rstd_ready = sem("r_rstd_ready")
        normed = sem("r_normed")
        turned = sem("r_turned")
        xt_copied = sem("r_xt_copied")
        xn_kept = sem("r_xn_kept")
        logits_done = sem("logits_done")
        logits_copied = sem("logits_copied")
        top_steps = sem("top_steps")
        top_kept = sem("top_kept")

        block = ctx.enter_context(nc.Block())

        @block.sync
        def _(sp):
            def step(t, p):
                if live(t - RING):
                    sp.wait_ge(normed, t - RING + 1)
                sp.dma_start(x2_in[:, p], at(x2_dram, t)).then_inc(x2_loaded[p], 16)
                if isinstance(t, int) and 4 <= t < 4 + E:
                    sp.dma_start(keep["down"][:, t - 4], down_w[t - 4].rearrange("(c p) n -> p c n", p=P))\
                        .then_inc(down_loaded, 16)

            run_steps(sp, step, 0, 12, 32, 31, RING)
            sp.wait_ge(down_loaded, 16 * E)

        @block.gpsimd
        def _(pool):
            nc.gpsimd.memset(power[:, :], -0.5).then_inc(power_ready, 1)
            pool.wait_ge(power_ready, 1)

            def step(t, p):
                pool.wait_ge(steps, 3 * t + 3)
                nc.gpsimd.tensor_tensor(rstd[:, :], var_eps[:, :], power[:, :], ALU.pow).then_inc(rstd_ready, 1)

            run_steps(pool, step, 0, 0, 32, 31)

        @block.vector
        def _(dve):
            nc.vector.memset(mark[:, :], 0.0)

            def norm_stats(t, p):
                dve.wait_ge(x2_loaded[p], landed(t, p, 16, RING))
                nc.vector.bn_stats(stats[:, :], x2_in[:, p]).then_inc(steps, 1)

            def norm_moments(t):
                wait_apart(nc, dve, steps, 3 * t + 1, mark)
                nc.vector.bn_aggr(moments[:, :], stats[:, :]).then_inc(steps, 1)

            def norm_var(t):
                dve.wait_ge(steps, 3 * t + 2)
                nc.vector.tensor_scalar(var_eps[:, :], moments[:, 1:2], LN_EPS, None, ALU.add).then_inc(steps, 1)

            def norm_apply(t, p):
                if live(t - 2):
                    dve.wait_ge(xn_kept, t - 1)
                dve.wait_ge(rstd_ready, t + 1)
                nc.vector.tensor_scalar(xn[:, p % 2], x2_in[:, p],
                                        moments[:, 0:1], rstd[:, :], ALU.subtract, ALU.mult).then_inc(normed, 1)

            def top(t, p):
                wait_apart(nc, dve, logits_copied, t + 1, mark, 2)
                nc.vector.max(top_val[:, p], logits[:, p]).then_inc(top_steps, 1)

            def top_index(t, p):
                wait_apart(nc, dve, top_steps, 2 * t + 1, mark, 3)
                nc.vector.max_index(top_idx[:, p], top_val[:, p], logits[:, p]).then_inc(top_steps, 1)

            def keep_top(t, p):
                dve.wait_ge(top_steps, 2 * t + 2)
                nc.vector.tensor_copy(keep["top_val"][:, column(t), :], top_val[:, p:p + 1, 0:TOP])\
                    .then_inc(top_kept, 1)
                nc.vector.tensor_copy(keep["top_idx"][:, column(t), :], top_idx[:, p:p + 1, 0:TOP])\
                    .then_inc(top_kept, 1)

            def step(b, p):
                new, old = live(b + 1), live(b - 2)
                if new:
                    norm_stats(b + 1, (p + 1) % RING)
                if old:
                    top(b - 2, p % 2)
                if new:
                    norm_moments(b + 1)
                if old:
                    top_index(b - 2, p % 2)
                if new:
                    norm_var(b + 1)
                if old:
                    keep_top(b - 2, p % 2)
                if new:
                    norm_apply(b + 1, (p + 1) % RING)

            run_steps(dve, step, -1, 3, 31, 33, RING)

        @block.scalar
        def _(act):
            def copy_xt(t, p):
                act.wait_ge(turned, t + 1)
                if live(t - 2):
                    act.wait_ge(logits_done, t - 1)
                nc.scalar.activation(xt[:, p], turn_ps[:, p].rearrange("k (c t) -> k c t", c=DC), ACT.Copy)\
                    .then_inc(xt_copied, 1)

            def keep_xn(t, p):
                nc.scalar.activation(keep["xn"][:, column(t), :], xn[:, p:p + 1], ACT.Copy).then_inc(xn_kept, 1)

            def copy_logits(t, p):
                act.wait_ge(logits_done, t + 1)
                if live(t - 2):
                    act.wait_ge(top_steps, 2 * (t - 1))
                nc.scalar.activation(logits[:, p], logit_ps[:, p, 0:E], ACT.Copy).then_inc(logits_copied, 1)

            def step(b, p):
                if live(b):
                    copy_xt(b, p)
                    keep_xn(b, p)
                if live(b - 1):
                    copy_logits(b - 1, 1 - p)

            run_steps(act, step, 0, 4, 32, 32)

        @block.tensor
        def _(pe):
            def turn(t, p):
                pe.wait_ge(normed, t + 1)
                if live(t - 2):
                    pe.wait_ge(xt_copied, t - 1)
                for c in range(DC):
                    last = nc.tensor.transpose(turn_ps[:, p, c * P:(c + 1) * P], xn[:, p, c * P:(c + 1) * P],
                                               keep["ident"][:, :])
                last.then_inc(turned, 1)

            def router(t, p):
                if isinstance(t, int) and t == 0:
                    pe.wait_ge(keep["weights_loaded"], keep["weights_count"])
                pe.wait_ge(xt_copied, t + 1)
                if live(t - 2):
                    pe.wait_ge(logits_copied, t - 1)
                for c in range(DC):
                    last = nc.tensor.matmul(logit_ps[:, p, 0:E], xt[:, p, c], keep["router"][:, c],
                                            start=(c == 0), stop=(c == DC - 1))
                last.then_inc(logits_done, 1)

            def step(b, p):
                if live(b):
                    turn(b, p)
                if live(b - 1):
                    router(b - 1, 1 - p)

            run_steps(pe, step, 0, 4, 32, 32)


EARLY = 18
PLAN_END = 5


class SharedExpert:

    def __init__(self, nc, ctx, name, tile_of, count, keep):
        sb = lambda part, shape: ctx.enter_context(nc.sbuf_tensor(f"{name}_{part}", shape, F32))
        ps = lambda part, shape: ctx.enter_context(nc.psum_tensor(f"{name}_{part}", shape, F32))
        sem = lambda part: ctx.enter_context(nc.semaphore(f"{name}_{part}"))
        self.nc, self.tile_of, self.count, self.keep = nc, tile_of, count, keep
        self.x = sb("x", [P, 1, D])
        self.xt = sb("xt", [P, DC, P])
        self.hid = sb("hid", [P, 2, F])
        self.hid_t = sb("hid_t", [P, FC, P])
        self.turn_ps = ps("turn_ps", [P, D])
        self.gu_ps = ps("gu_ps", [P, 2, 2 * F])
        self.ht_ps = ps("ht_ps", [P, 2, 512])
        self.down_ps = ps("down_ps", [P, 2, D])
        self.x_placed = sem("x_placed")
        self.turned = sem("turned")
        self.xt_copied = sem("xt_copied")
        self.gu_done = sem("gu_done")
        self.gated = sem("gated")
        self.hid_done = sem("hid_done")
        self.hid_turned = sem("hid_turned")
        self.hid_copied = sem("hid_copied")
        self.down_done = sem("down_done")
        self.acc_done = sem("acc_done")

    def scalar_start(self):
        self.place_x(0)

    def scalar_step(self, act, j, p):
        if live(j, self.count):
            self.silu(act, j, p)
        if live(j + 1, self.count):
            self.copy_xt(act, j + 1)
        if live(j + 2, self.count):
            self.place_x(j + 2)
        if live(j, self.count):
            self.copy_hidden(act, j, p)

    def place_x(self, j):
        self.nc.scalar.activation(self.x[:, :, :], self.keep["xn"][:, column(self.tile_of(j)), :], ACT.Copy)\
            .then_inc(self.x_placed, 1)

    def silu(self, act, j, p):
        act.wait_ge(self.gu_done, j + 1)
        if live(j - 2):
            act.wait_ge(self.hid_turned, j - 1)
        self.nc.scalar.activation(self.hid[:, p], self.gu_ps[:, p, 0:F], ACT.Silu).then_inc(self.gated, 1)

    def copy_xt(self, act, j):
        act.wait_ge(self.turned, j + 1)
        if live(j - 1):
            act.wait_ge(self.gu_done, j)
        self.nc.scalar.activation(self.xt[:, :, :], self.turn_ps[:, :].rearrange("k (c t) -> k c t", c=DC),
                                  ACT.Copy).then_inc(self.xt_copied, 1)

    def copy_hidden(self, act, j, p):
        act.wait_ge(self.hid_turned, j + 1)
        if live(j - 1):
            act.wait_ge(self.down_done, j)
        self.nc.scalar.activation(self.hid_t[:, :, :], self.ht_ps[:, p, 0:F].rearrange("k (c t) -> k c t", c=FC),
                                  ACT.Copy).then_inc(self.hid_copied, 1)

    def hidden(self, dve, j, p):
        dve.wait_ge(self.gated, j + 1)
        self.nc.vector.tensor_tensor(self.hid[:, p], self.hid[:, p], self.gu_ps[:, p, F:], ALU.mult)\
            .then_inc(self.hid_done, 1)

    def tensor_step(self, pe, j, p, between=None):
        if live(j, self.count):
            self.gate_up(pe, j, p)
        if live(j + 1, self.count):
            self.turn(pe, j + 1)
        if between:
            between()
        if live(j - 1, self.count):
            self.down(pe, j - 1, 1 - p)
        if live(j, self.count):
            self.turn_hidden(pe, j, p)

    def turn(self, pe, j):
        pe.wait_ge(self.x_placed, j + 1)
        if live(j - 1):
            pe.wait_ge(self.xt_copied, j)
        for c in range(DC):
            last = self.nc.tensor.transpose(self.turn_ps[:, c * P:(c + 1) * P], self.x[:, 0, c * P:(c + 1) * P],
                                            self.keep["ident"][:, :])
        last.then_inc(self.turned, 1)

    def gate_up(self, pe, j, p):
        pe.wait_ge(self.xt_copied, j + 1)
        if live(j - 2):
            pe.wait_ge(self.hid_done, j - 1)
        for c in range(DC):
            last = self.nc.tensor.matmul(self.gu_ps[:, p], self.xt[:, c], self.keep["shared_gu"][:, c],
                                         start=(c == 0), stop=(c == DC - 1))
        last.then_inc(self.gu_done, 1)

    def turn_hidden(self, pe, j, p):
        pe.wait_ge(self.hid_done, j + 1)
        if live(j - 2):
            pe.wait_ge(self.hid_copied, j - 1)
        for c in range(FC):
            last = self.nc.tensor.transpose(self.ht_ps[:, p, c * P:(c + 1) * P],
                                            self.hid[:, p, c * P:(c + 1) * P], self.keep["ident"][:, :])
        last.then_inc(self.hid_turned, 1)

    def down(self, pe, j, p):
        pe.wait_ge(self.hid_copied, j + 1)
        if live(j - 2):
            pe.wait_ge(self.acc_done, j - 1)
        for c in range(FC):
            last = self.nc.tensor.matmul(self.down_ps[:, p], self.hid_t[:, c], self.keep["shared_down"][:, c],
                                         start=(c == 0), stop=(c == FC - 1))
        last.then_inc(self.down_done, 1)


def dispatch(nc, x2_dram, acc_dram, keep):
    RING = 4
    SLOTS = 3
    MAXT = T // P
    xn = keep["xn"]
    rows_dram = keep["rows_dram"]
    with ExitStack() as ctx:
        sb = lambda name, shape, dt: ctx.enter_context(nc.sbuf_tensor(name, shape, dt))
        ps = lambda name, shape, dt: ctx.enter_context(nc.psum_tensor(name, shape, dt))
        sem = lambda name: ctx.enter_context(nc.semaphore(name))

        iota_e = sb("p_iota_e", [P, E], I32)
        iota_k = sb("p_iota_k", [P, MAXT], I32)
        iota_t = sb("p_iota_t", [P, TILES], I32)
        num_e = sb("p_num_e", [P, 1, E], F32)
        num_k = sb("p_num_k", [P, 1, MAXT], F32)
        num_t = sb("p_num_t", [P, TILES, 1], F32)
        ones = sb("p_ones", [P, P], BF16)
        before = sb("p_before", [P, P], BF16)
        chosen = sb("p_chosen", [P, TOP, B, E], BF16)
        either = sb("p_either", [P, B, E], BF16)
        count = sb("p_count", [P, B, E], F32)
        pos = sb("p_pos", [P, TOP, B], F32)
        over = sb("p_over", [P, E, MAXT], BF16)
        tiles = sb("p_tiles", [P, E], F32)
        ends = sb("p_ends", [P, 2, E], F32)
        starts = sb("p_starts", [P, 1, E], F32)
        passed = sb("p_passed", [P, TILES, E], BF16)
        owner = sb("p_owner", [P, TILES], F32)
        plan_ps = ps("p_plan_ps", [P, 2, B * E], F32)

        x2 = sb("s_x2", [P, RING, D], F32)
        scaled = sb("s_scaled", [P, SLOTS, TOP, D], F32)
        upto, place = (scaled[:, SLOTS - 1, k].rearrange("p (a b e) -> p a b e", a=2, b=B) for k in range(TOP))

        iotas = sem("iotas")
        masks = sem("masks")
        chain = sem("plan_chain")
        ranked = sem("ranked")
        prob_done = sem("prob_done")
        x2_loaded = [sem(f"s_x2_loaded{k}") for k in range(RING)]
        acc_written = sem("s_acc_written")
        row_scaled = sem("s_row_scaled")
        scattered = [sem(f"s_scattered{k}") for k in range(SLOTS)]
        tile_of = lambda j: j + EARLY - PLAN_END if isinstance(j, int) and j < PLAN_END else j - PLAN_END
        shared = SharedExpert(nc, ctx, "s", tile_of, EARLY, keep)

        block = ctx.enter_context(nc.Block())

        @block.sync
        def _(sp):
            def load(j, p):
                if isinstance(j, int) and RING <= j < RING + PLAN_END:
                    sp.wait_ge(acc_written, 16 * (j - RING + 1))
                elif live(j - RING):
                    sp.wait_ge(shared.acc_done, j - RING + 1)
                sp.dma_start(x2[:, p], at(x2_dram, tile_of(j))).then_inc(x2_loaded[p], 16)

            def write(j, p):
                sp.wait_ge(shared.acc_done, j + 1)
                if j > 0:
                    sp.wait_ge(acc_written, 16 * j)
                sp.dma_start(acc_dram[j], x2[:, p]).then_inc(acc_written, 16)

            def step(j, p):
                if isinstance(j, int) and 0 <= j < PLAN_END:
                    write(j, p)
                if live(j + 3, EARLY):
                    load(j + 3, (p + 3) % RING)

            run_steps(sp, step, -3, 7, EARLY - 3, EARLY - 1, RING)
            sp.wait_ge(acc_written, 16 * PLAN_END)

        @block.gpsimd
        def _(pool):
            nc.gpsimd.iota(iota_e[:, :], pattern=[[1, E]], base=0, channel_multiplier=0).then_inc(iotas, 1)
            nc.gpsimd.iota(iota_k[:, :], pattern=[[P, MAXT]], base=0, channel_multiplier=0).then_inc(iotas, 1)
            nc.gpsimd.iota(iota_t[:, :], pattern=[[1, TILES]], base=0, channel_multiplier=0).then_inc(iotas, 1)
            nc.gpsimd.memset(ones[:, :], 1.0).then_inc(masks, 1)
            nc.gpsimd.memset(before[:, :], 1.0).then_inc(masks, 1)
            pool.wait_ge(masks, 2)
            nc.gpsimd.affine_select(out=before[:, :], in_=before[:, :], compare_op=ALU.is_gt, fill=0.0,
                                    base=0, pattern=[[1, P]], channel_multiplier=-1).then_inc(masks, 1)
            for t in range(B):
                pool.wait_ge(row_scaled, TOP * (t + 1))
                for k in range(TOP):
                    nc.gpsimd.indirect_dma_start(
                        out=rows_dram,
                        out_offset=bass.IndirectOffsetOnAxis(ap=keep["place"][:, t, k:k + 1], axis=0),
                        in_=scaled[:, t % SLOTS, k], in_offset=None).then_inc(scattered[t % SLOTS], 16)
            drain_ring(pool, scattered, B, 16 * TOP)

        @block.vector
        def _(dve):
            V = nc.vector
            done = [0]

            def then(instruction):
                done[0] += 1
                instruction.then_inc(chain, 1)
                dve.wait_ge(chain, done[0])

            def plan_choices():
                dve.wait_ge(iotas, 3)
                then(V.tensor_copy(num_e[:, 0, :], iota_e[:, :]))
                then(V.tensor_copy(num_k[:, 0, :], iota_k[:, :]))
                then(V.tensor_copy(num_t[:, :, 0], iota_t[:, :]))
                for k in range(TOP):
                    then(V.tensor_tensor(chosen[:, k], keep["top_idx"][:, :, k:k + 1].broadcast_to([P, B, E]),
                                         num_e[:, :, :].broadcast_to([P, B, E]), ALU.is_equal))
                then(V.tensor_tensor(either[:, :, :], chosen[:, 0], chosen[:, 1], ALU.add))

            def plan_running_counts():
                dve.wait_ge(ranked, 1)
                counts = plan_ps[:, 1].rearrange("p (b e) -> p b e", b=B)
                then(V.tensor_copy(count[:, :, :], counts))
                then(V.tensor_copy(upto[:, 0], counts))
                now, shift = 0, 1
                while shift < B:
                    then(V.tensor_tensor(upto[:, 1 - now, shift:], upto[:, now, shift:], upto[:, now, :B - shift],
                                         ALU.add))
                    then(V.tensor_copy(upto[:, 1 - now, :shift], upto[:, now, :shift]))
                    now, shift = 1 - now, 2 * shift
                return now

            def plan_tiles(now):
                total = upto[:, now, B - 1:B, :].rearrange("p o e -> p e o")
                then(V.tensor_tensor(over[:, :, :], total.broadcast_to([P, E, MAXT]),
                                     num_k[:, :, :].broadcast_to([P, E, MAXT]), ALU.is_gt))
                then(V.tensor_reduce(tiles[:, :], over[:, :, :], AX.X, ALU.add))

            def plan_ends():
                then(V.tensor_copy(ends[:, 0], tiles[:, :]))
                cur, shift = 0, 1
                while shift < E:
                    then(V.tensor_tensor(ends[:, 1 - cur, shift:], ends[:, cur, shift:],
                                         ends[:, cur, :E - shift], ALU.add))
                    then(V.tensor_copy(ends[:, 1 - cur, :shift], ends[:, cur, :shift]))
                    cur, shift = 1 - cur, 2 * shift
                then(V.tensor_tensor(starts[:, 0, :], ends[:, cur], tiles[:, :], ALU.subtract))
                then(V.tensor_scalar(starts[:, 0, :], starts[:, 0, :], float(P), None, ALU.mult))
                return cur

            def plan_places(now):
                then(V.tensor_tensor(place[:, 0], upto[:, now], count[:, :, :], ALU.subtract))
                then(V.tensor_tensor(place[:, 1], place[:, 0], starts[:, :, :].broadcast_to([P, B, E]), ALU.add))
                then(V.tensor_tensor(place[:, 0], place[:, 1], plan_ps[:, 0].rearrange("p (b e) -> p b e", b=B),
                                     ALU.add))

            def plan_pick(k):
                then(V.tensor_tensor(upto[:, k], chosen[:, k], place[:, 0], ALU.mult))
                then(V.tensor_reduce(pos[:, k], upto[:, k], AX.X, ALU.add))
                then(V.tensor_copy(keep["place"][:, :, k], pos[:, k]))

            def plan_owners(cur):
                then(V.tensor_tensor(passed[:, :, :], num_t[:, :, :].broadcast_to([P, TILES, E]),
                                     ends[:, cur:cur + 1, :].broadcast_to([P, TILES, E]), ALU.is_ge))
                then(V.tensor_reduce(owner[:, :], passed[:, :, :], AX.X, ALU.add))
                then(V.tensor_scalar(keep["owner"][:, :], owner[:, :], float(E - 1), None, ALU.min))

            def scale(n, slot):
                t = n * SLOTS + slot
                if isinstance(t, int) and t == 0:
                    dve.wait_ge(prob_done, 1)
                if not (isinstance(n, int) and n == 0):
                    dve.wait_ge(scattered[slot], 16 * TOP * n)
                for k in range(TOP):
                    prob = keep["prob"][:, column(t), k:k + 1].rearrange("p o k -> p (o k)")
                    V.tensor_scalar(scaled[:, slot, k], xn[:, column(t), :].rearrange("p o d -> p (o d)"), prob,
                                    None, ALU.mult).then_inc(row_scaled, 1)

            def accumulate(j, p):
                dve.wait_ge(shared.down_done, j + 1)
                dve.wait_ge(x2_loaded[p], landed(j, p, 16, RING))
                if isinstance(j, int) and j < PLAN_END:
                    total = x2[:, p:p + 1]
                else:
                    dve.wait_ge(row_scaled, TOP * (j - PLAN_END + 1))
                    total = xn[:, column(tile_of(j)), :]
                V.tensor_tensor(total, x2[:, p:p + 1], shared.down_ps[:, p % 2:p % 2 + 1], ALU.add)\
                    .then_inc(shared.acc_done, 1)

            def step(b, p):
                if live(b, EARLY):
                    shared.hidden(dve, b, p % 2)
                if live(b - 1):
                    accumulate(b - 1, (p - 1) % RING)

            def step_and_scale(b, p):
                step(b, p)
                for slot in range(SLOTS):
                    if live((b - PLAN_END) * SLOTS + slot):
                        scale(b - PLAN_END, slot)

            step(0, 0)
            plan_choices()
            step(1, 1)
            now = plan_running_counts()
            step(2, 2)
            plan_tiles(now)
            cur = plan_ends()
            step(3, 3)
            plan_places(now)
            for k in range(TOP):
                plan_pick(k)
            step(4, 0)
            plan_owners(cur)
            run_steps(dve, step_and_scale, PLAN_END, PLAN_END + 2, PLAN_END + 10, EARLY, RING)

        @block.scalar
        def _(act):
            nc.scalar.activation(keep["prob"][:, :, :], keep["top_val"][:, :, :], ACT.Sigmoid).then_inc(prob_done, 1)
            shared.scalar_start()
            run_steps(act, lambda j, p: shared.scalar_step(act, j, p), -1, 3, EARLY - 3, EARLY - 1)

        @block.tensor
        def _(pe):
            def rank():
                pe.wait_ge(masks, 3)
                pe.wait_ge(chain, 6)
                flags = either[:, :, :].rearrange("p b e -> p (b e)")
                nc.tensor.matmul(plan_ps[:, 0], before[:, :], flags, start=True, stop=True)
                nc.tensor.matmul(plan_ps[:, 1], ones[:, :], flags, start=True, stop=True).then_inc(ranked, 1)

            def step(j, p):
                shared.tensor_step(pe, j, p, rank if isinstance(j, int) and j == 1 else None)

            run_steps(pe, step, -1, 3, EARLY - 1, EARLY)


def experts(nc, y_dram, keep):
    RING = 4
    rows = keep["rows_dram"].rearrange("(i p) d -> i p d", p=P)
    N = TILES
    with ExitStack() as ctx:
        sb = lambda name, shape, dt: ctx.enter_context(nc.sbuf_tensor(name, shape, dt))
        ps = lambda name, shape, dt: ctx.enter_context(nc.psum_tensor(name, shape, dt))
        sem = lambda name: ctx.enter_context(nc.semaphore(name))

        x = sb("e_x", [P, RING, D], F32)
        xt = sb("e_xt", [P, 2, DC, P], F32)
        gate = sb("e_gate", [P, 2, F], F32)
        hid = sb("e_hid", [P, 2, F], F32)
        hid_t = sb("e_hid_t", [P, 2, FC, P], F32)
        y = sb("e_y", [P, 2, D], F32)
        turn_ps = ps("e_turn_ps", [P, D], F32)
        gu_ps = ps("e_gu_ps", [P, 2, 2 * F], F32)
        ht_ps = ps("e_ht_ps", [P, 2, 512], F32)
        down_ps = ps("e_down_ps", [P, 2, D], F32)

        x_loaded = [sem(f"e_x_loaded{k}") for k in range(RING)]
        turned = sem("e_turned")
        xt_copied = sem("e_xt_copied")
        gu_done = sem("e_gu_done")
        gated = sem("e_gated")
        hid_done = sem("e_hid_done")
        hid_turned = sem("e_hid_turned")
        hid_copied = sem("e_hid_copied")
        down_done = sem("e_down_done")
        y_done = sem("e_y_done")
        y_written = [sem(f"e_y_written{k}") for k in range(2)]

        block = ctx.enter_context(nc.Block())

        @block.sync
        def _(sp):
            def step(i, p):
                if live(i + 3, N):
                    if live(i - 1, N):
                        sp.wait_ge(turned, i)
                    sp.dma_start(x[:, (p + 3) % RING], at(rows, i + 3)).then_inc(x_loaded[(p + 3) % RING], 16)
                if live(i, N):
                    sp.wait_ge(y_done, i + 1)
                    sp.dma_start(at(y_dram, i), y[:, p % 2]).then_inc(y_written[p % 2], 16)

            run_steps(sp, step, -3, 4, N - 3, N - 1, RING)
            drain_ring(sp, y_written, N)

        @block.vector
        def _(dve):
            def hidden(t, p):
                dve.wait_ge(gated, t + 1)
                if live(t - 2, N):
                    dve.wait_ge(hid_turned, t - 1)
                nc.vector.tensor_tensor(hid[:, p], gate[:, p], gu_ps[:, p, F:], ALU.mult).then_inc(hid_done, 1)

            def copy_hidden(t, p):
                dve.wait_ge(hid_turned, t + 1)
                if live(t - 2, N):
                    dve.wait_ge(down_done, t - 1)
                nc.vector.tensor_copy(hid_t[:, p], ht_ps[:, p, 0:F].rearrange("k (c t) -> k c t", c=FC))\
                    .then_inc(hid_copied, 1)

            def copy_y(t, p):
                dve.wait_ge(down_done, t + 1)
                if live(t - 2, N):
                    dve.wait_ge(y_written[p], landed(t - 2, p))
                nc.vector.tensor_copy(y[:, p], down_ps[:, p]).then_inc(y_done, 1)

            def step(i, p):
                if live(i, N):
                    hidden(i, p)
                if live(i - 1, N):
                    copy_y(i - 1, 1 - p)
                if live(i, N):
                    copy_hidden(i, p)

            run_steps(dve, step, 0, 4, N - 1, N)

        @block.scalar
        def _(act):
            def copy_xt(t, p):
                act.wait_ge(turned, t + 1)
                if live(t - 2, N):
                    act.wait_ge(gu_done, t - 1)
                nc.scalar.activation(xt[:, p], turn_ps[:, :].rearrange("k (c t) -> k c t", c=DC), ACT.Copy)\
                    .then_inc(xt_copied, 1)

            def silu(t, p):
                act.wait_ge(gu_done, t + 1)
                if live(t - 2, N):
                    act.wait_ge(hid_done, t - 1)
                nc.scalar.activation(gate[:, p], gu_ps[:, p, 0:F], ACT.Silu).then_inc(gated, 1)

            def step(i, p):
                if live(i, N):
                    silu(i, p)
                if live(i + 1, N):
                    copy_xt(i + 1, 1 - p)

            run_steps(act, step, -1, 3, N - 2, N - 1)

        @block.tensor
        def _(pe):
            def owner(t):
                return pe.value_load(keep["owner"][0:1, column(t)], min_val=0, max_val=E - 1)

            def turn(t, p):
                pe.wait_ge(x_loaded[p], landed(t, p, 16, RING))
                if live(t - 1, N):
                    pe.wait_ge(xt_copied, t)
                for c in range(DC):
                    last = nc.tensor.transpose(turn_ps[:, c * P:(c + 1) * P], x[:, p, c * P:(c + 1) * P],
                                               keep["ident"][:, :])
                last.then_inc(turned, 1)

            def gate_up(t, p):
                e = owner(t)
                pe.wait_ge(xt_copied, t + 1)
                if live(t - 2, N):
                    pe.wait_ge(hid_done, t - 1)
                for c in range(DC):
                    last = nc.tensor.matmul(gu_ps[:, p], xt[:, p, c],
                                            keep["gate_up"][:, bass.ds(e * (DC * 2 * F) + c * 2 * F, 2 * F)],
                                            start=(c == 0), stop=(c == DC - 1))
                last.then_inc(gu_done, 1)

            def turn_hidden(t, p):
                pe.wait_ge(hid_done, t + 1)
                if live(t - 2, N):
                    pe.wait_ge(hid_copied, t - 1)
                for c in range(FC):
                    last = nc.tensor.transpose(ht_ps[:, p, c * P:(c + 1) * P], hid[:, p, c * P:(c + 1) * P],
                                               keep["ident"][:, :])
                last.then_inc(hid_turned, 1)

            def down(t, p):
                e = owner(t)
                pe.wait_ge(hid_copied, t + 1)
                if live(t - 2, N):
                    pe.wait_ge(y_done, t - 1)
                for c in range(FC):
                    last = nc.tensor.matmul(down_ps[:, p], hid_t[:, p, c],
                                            keep["down_flat"][:, bass.ds(e * (FC * D) + c * D, D)],
                                            start=(c == 0), stop=(c == FC - 1))
                last.then_inc(down_done, 1)

            def step(i, p):
                if live(i, N):
                    gate_up(i, p % 2)
                if live(i + 1, N):
                    turn(i + 1, (p + 1) % RING)
                if live(i - 1, N):
                    down(i - 1, (p + 1) % 2)
                if live(i, N):
                    turn_hidden(i, p % 2)

            run_steps(pe, step, -1, 4, N - 3, N, RING)


def combine(nc, x2_dram, acc_dram, y_dram, out, keep):
    RING = 4
    Y_RING = 2 * RING
    LATE = B - EARLY
    total = keep["xn"]
    y_rows = y_dram.rearrange("i p d -> (i p) d")
    with ExitStack() as ctx:
        sb = lambda name, shape, dt: ctx.enter_context(nc.sbuf_tensor(name, shape, dt))
        sem = lambda name: ctx.enter_context(nc.semaphore(name))
        x2 = sb("c_x2", [P, RING, D], F32)
        y = sb("c_y", [P, Y_RING, TOP, D], F32)
        acc_loaded = sem("c_acc_loaded")
        x2_loaded = [sem(f"c_x2_loaded{k}") for k in range(RING)]
        gathered = [sem(f"c_gathered{k}") for k in range(Y_RING)]
        summed = sem("c_summed")
        out_done = sem("c_out_done")
        out_written = sem("c_out_written")
        shared = SharedExpert(nc, ctx, "c", lambda j: j + EARLY, LATE, keep)

        block = ctx.enter_context(nc.Block())

        @block.sync
        def _(sp):
            def load(j, p):
                if live(j - RING):
                    sp.wait_ge(shared.acc_done, j - RING + 1)
                sp.dma_start(x2[:, p], at(x2_dram, EARLY + j)).then_inc(x2_loaded[p], 16)

            def write(t):
                sp.wait_ge(out_done, t + 1)
                sp.dma_start(at(out, t), total[:, column(t), :]).then_inc(out_written, 16)

            def step(j, p):
                if live(j + 3, LATE):
                    load(j + 3, (p + 3) % RING)
                for k in range(2):
                    if live(2 * j + k):
                        write(2 * j + k)

            sp.dma_start(total[:, EARLY - PLAN_END:EARLY], acc_dram.rearrange("b p d -> p b d"))\
                .then_inc(acc_loaded, 16)
            run_steps(sp, step, -3, 3, LATE - 3, B // 2 - 1, RING)
            sp.wait_ge(out_written, 16 * B)

        @block.gpsimd
        def _(pool):
            for t in range(B):
                if live(t - Y_RING):
                    pool.wait_ge(out_done, t - Y_RING + 1)
                for k in range(TOP):
                    nc.gpsimd.indirect_dma_start(
                        out=y[:, t % Y_RING, k], out_offset=None, in_=y_rows,
                        in_offset=bass.IndirectOffsetOnAxis(ap=keep["place"][:, t, k:k + 1], axis=0))\
                        .then_inc(gathered[t % Y_RING], 16)

        @block.vector
        def _(dve):
            def accumulate(j, p):
                dve.wait_ge(shared.down_done, j + 1)
                dve.wait_ge(x2_loaded[p], landed(j, p, 16, RING))
                nc.vector.tensor_tensor(total[:, column(EARLY + j), :], x2[:, p:p + 1],
                                        shared.down_ps[:, p % 2:p % 2 + 1], ALU.add).then_inc(shared.acc_done, 1)

            def finish(t, p, late):
                dve.wait_ge(gathered[p], landed(t, p, 32, Y_RING))
                nc.vector.tensor_tensor(y[:, p, 0], y[:, p, 0], y[:, p, 1], ALU.add).then_inc(summed, 1)
                if late:
                    dve.wait_ge(shared.acc_done, t - EARLY + 1)
                dve.wait_ge(summed, t + 1)
                nc.vector.tensor_tensor(total[:, column(t), :], total[:, column(t), :], y[:, p:p + 1, 0], ALU.add)\
                    .then_inc(out_done, 1)

            def step(j, p, late):
                if live(j, LATE):
                    shared.hidden(dve, j, p % 2)
                if live(j - 1, LATE):
                    accumulate(j - 1, (p - 1) % RING)
                for k in range(2):
                    finish(2 * j + k, 2 * p + k, late)

            dve.wait_ge(acc_loaded, 16)
            run_steps(dve, lambda j, p: step(j, p, False), 0, 1, EARLY // 2, EARLY // 2 - 1, RING)
            run_steps(dve, lambda j, p: step(j, p, True), EARLY // 2, EARLY // 2, LATE - 1, B // 2 - 1,
                      RING)

        @block.scalar
        def _(act):
            shared.scalar_start()
            run_steps(act, lambda j, p: shared.scalar_step(act, j, p), -1, 3, LATE - 3, LATE - 1)

        @block.tensor
        def _(pe):
            run_steps(pe, lambda j, p: shared.tensor_step(pe, j, p), -1, 3, LATE - 1, LATE)


def program(nc, x, ctx_2048, itok_B_779_1933, router_w, gate_up_w, down_w, shared_gate_w, shared_up_w,
            shared_down_w, out):
    scr = lambda name, shape: nc.dram_tensor(name, shape, F32, kind="Internal").ap()
    x2_dram = scr("x2_dram", [B, P, D])
    acc_dram = scr("acc_dram", [PLAN_END, P, D])
    y_dram = scr("y_dram", [TILES, P, D])
    with ExitStack() as ctx:
        sb = lambda name, shape, dt: ctx.enter_context(nc.sbuf_tensor(name, shape, dt))
        gate_up = sb("gate_up", [P, E * DC * 2 * F], F32)
        shared_gu = sb("shared_gu", [P, DC, 2 * F], F32)
        shared_down = sb("shared_down", [P, FC, D], F32)
        router = sb("router", [P, DC, E], F32)
        keep = {
            "rows_dram": scr("rows_dram", [TILES * P, D]),
            "ident": sb("ident", [P, P], F32),
            "router": router,
            "shared_gu": shared_gu,
            "shared_down": shared_down,
            "gate_up": gate_up,
            "weights_loaded": ctx.enter_context(nc.semaphore("weights_loaded")),
        }
        gu_e = gate_up[:, :].rearrange("p (e c n) -> p e c n", e=E, c=DC)
        keep["weight_loads"] = [(gu_e[:, e], gate_up_w[e].rearrange("(c p) n -> p c n", p=P)) for e in range(E)]
        keep["weight_loads"] += [
            (shared_gu[:, :, 0:F], shared_gate_w.rearrange("(c p) n -> p c n", p=P)),
            (shared_gu[:, :, F:], shared_up_w.rearrange("(c p) n -> p c n", p=P)),
            (shared_down[:, :, :], shared_down_w.rearrange("(c p) n -> p c n", p=P)),
            (router[:, :, :], router_w.rearrange("(c p) n -> p c n", p=P))]
        keep["weights_count"] = 16 * len(keep["weight_loads"])
        attention(nc, x, ctx_2048, itok_B_779_1933, x2_dram, keep)
        keep["top_val"] = sb("top_val_all", [P, B, TOP], F32)
        keep["top_idx"] = sb("top_idx_all", [P, B, TOP], F32)
        keep["prob"] = sb("prob_all", [P, B, TOP], F32)
        keep["place"] = sb("place_all", [P, B, TOP], U32)
        keep["owner"] = sb("owner_all", [P, TILES], I32)
        keep["xn"] = sb("xn_all", [P, B, D], F32)
        with nc.sbuf_tensor("down", [P, E * FC * D], F32) as down_flat:
            keep["down_flat"] = down_flat
            keep["down"] = down_flat[:, :].rearrange("p (e c n) -> p e c n", e=E, c=FC)
            route(nc, x2_dram, down_w, keep)
            dispatch(nc, x2_dram, acc_dram, keep)
            experts(nc, y_dram, keep)
        combine(nc, x2_dram, acc_dram, y_dram, out, keep)


_INS = ["x", "ctx_2048", "itok_B_779_1933", "L0_ffn_router_w", "L0_ffn_gate_up_w", "L0_ffn_down_w",
        "L0_ffn_shared_gate_w", "L0_ffn_shared_up_w", "L0_ffn_shared_down_w"]
_OUTS = [((B, ROWS, L), "float32")]


def kernel(**inputs):
    import numpy as _np
    import concourse.bacc as _bacc
    from concourse import mybir as _mybir
    from concourse.bass_utils import run_bass_kernel_spmd as _run

    nc = _bacc.Bacc("TRN2", target_bir_lowering=False, num_devices=1)
    arrays, args = {}, []
    for name in _INS:
        a = _np.ascontiguousarray(inputs[name])
        arrays[f"in_{name}_dram"] = a
        args.append(nc.dram_tensor(f"in_{name}_dram", a.shape, _mybir.dt.from_np(a.dtype), kind="ExternalInput").ap())
    for i, (shape, dtype) in enumerate(_OUTS):
        dt = _mybir.dt.from_np(_np.dtype(dtype))
        args.append(nc.dram_tensor(f"out_{i}_dram", shape, dt, kind="ExternalOutput").ap())
    program(nc, *args)
    r = _run(nc, [arrays], core_ids=[0])
    got = tuple(r.results[0][f"out_{i}_dram"] for i in range(len(_OUTS)))
    return got[0]
```
